# Optimizing a Trainium2 kernel written in Bass

```python
import numpy as np
import jax
import jax.numpy as jnp

def _softmax(x, axis=-1):
    return jax.nn.softmax(x, axis=axis)

def _gelu(x):
    return jax.nn.gelu(x, approximate=True)

def _silu(x):
    return jax.nn.silu(x)

def _sigmoid(x):
    return jax.nn.sigmoid(x)

def _layernorm(x, axis=-1, eps=1e-05):
    m = jnp.mean(x, axis=axis, keepdims=True)
    v = jnp.var(x, axis=axis, keepdims=True)
    return (x - m) / jnp.sqrt(v + eps)

def _scatter_add(tgt, idx, src, axis=0):
    return tgt.at[idx].add(src)

def _segment_sum(src, seg, n):
    return jax.ops.segment_sum(src, seg, n)
kernel_name = 'mk_decoder_postln_d1_seqx_r4_3c0ffb'

def setup_inputs(seed: int=0):
    np.random.seed(seed)
    _w = jnp.asarray

    def _rec_inputs():
        import jax
        import jax.numpy as jnp
        _rk = jax.random.key(seed)
        x = -0.0002928 + 1 * jax.random.normal(jax.random.fold_in(_rk, 1), (16, 512, 256), jnp.float32)
        _lenS = 512 - jax.random.randint(jax.random.fold_in(_rk, 7), (16,), 0, max(1, 512 // 4) + 1, jnp.int32)
        _lenS2 = 64 - jax.random.randint(jax.random.fold_in(_rk, 8), (16,), 0, max(1, 64 // 4) + 1, jnp.int32)
        _ctx_512P = jax.random.normal(jax.random.fold_in(_rk, 11), (16, 16, 128), jnp.float32)
        _ctx_512c = jax.random.dirichlet(jax.random.fold_in(_rk, 511), 0.3 * jnp.ones((16,), jnp.float32), (16, 64))
        _ctx_512t = jnp.einsum('bsk,bkd->bsd', _ctx_512c, _ctx_512P)
        _ctx_512t = _ctx_512t * jax.lax.rsqrt(jnp.mean(jnp.square(_ctx_512t)) + 1e-12) * 0.953939
        ctx_512 = 0.00222621 + 0.99962 * (_ctx_512t + 0.3 * jax.random.normal(jax.random.fold_in(_rk, 611), (16, 64, 128), jnp.float32))
        return (x, ctx_512)
    x, ctx_512 = _rec_inputs()

    def _L0_attn_setup():
        import jax, jax.numpy as jnp
        import numpy as np
        B, L, D, S, K, FF = (2, 1024, 256, 16, 3, 672)
        EPS = 1e-06

        def rmsnorm(x, w):
            var = jnp.mean(x * x, axis=-1, keepdims=True)
            return x * jax.lax.rsqrt(var + EPS) * w
        key = jax.random.key(seed)
        ks = jax.random.split(key, 12)
        return {'u': jax.random.normal(ks[0], (B, L, D), jnp.float32), 'pre_norm_w': jnp.ones((D,), jnp.float32), 'in_proj_w': jax.random.normal(ks[1], (3 * D, D), jnp.float32) * D ** (-0.5), 'short_w': jax.random.normal(ks[2], (3 * D, 1, K), jnp.float32) * 0.3, 'short_b': jax.random.normal(ks[3], (3 * D,), jnp.float32) * 0.02, 'log_poles': -(jax.random.uniform(ks[4], (D, S, 1), jnp.float32) * 0.3 + 0.001), 'residues': jax.random.normal(ks[5], (D, S), jnp.float32) * S ** (-0.5), 'D_skip': jax.random.normal(ks[6], (D,), jnp.float32) * 0.02, 'out_proj_w': jax.random.normal(ks[7], (D, D), jnp.float32) * D ** (-0.5), 'post_norm_w': jnp.ones((D,), jnp.float32), 'l1_w': jax.random.normal(ks[8], (FF, D), jnp.float32) * D ** (-0.5), 'l2_w': jax.random.normal(ks[9], (FF, D), jnp.float32) * D ** (-0.5), 'l3_w': jax.random.normal(ks[10], (D, FF), jnp.float32) * FF ** (-0.5)}
    _L0_attn_all = _L0_attn_setup()
    _L0_attn_in = {k: v for k, v in _L0_attn_all.items() if k in ('pre_norm_w', 'in_proj_w', 'short_w', 'short_b', 'log_poles', 'residues', 'D_skip', 'out_proj_w', 'post_norm_w', 'l1_w', 'l2_w', 'l3_w')}
    del _L0_attn_all

    def _L0_xattn_setup():
        import jax, jax.numpy as jnp
        import numpy as np
        B, T, TC, C, CC, H = (2, 512, 128, 256, 128, 16)
        D = C // H

        def _heads(t):
            b, l, _ = t.shape
            return t.reshape(b, l, H, D).transpose(0, 2, 1, 3)
        key = jax.random.key(seed)
        ks = jax.random.split(key, 18)
        w = lambda k, i, o: jax.random.normal(k, (i, o), jnp.float32) / np.sqrt(i).astype(np.float32)
        return {'x': jax.random.normal(ks[0], (B, T, C), jnp.float32), 'cross_input': jax.random.normal(ks[1], (B, TC, CC), jnp.float32), 'Wk': w(ks[2], C, C), 'bk': jnp.zeros((C,), jnp.float32), 'Wq': w(ks[3], C, C), 'bq': jnp.zeros((C,), jnp.float32), 'Wv': w(ks[4], C, C), 'bv': jnp.zeros((C,), jnp.float32), 'Wck': w(ks[5], CC, C), 'bck': jnp.zeros((C,), jnp.float32), 'Wcq': w(ks[6], C, C), 'bcq': jnp.zeros((C,), jnp.float32), 'Wcv': w(ks[7], CC, C), 'bcv': jnp.zeros((C,), jnp.float32), 'Wp': w(ks[8], C, C), 'bp': jnp.zeros((C,), jnp.float32)}
    _L0_xattn_all = _L0_xattn_setup()
    _L0_xattn_in = {k: v for k, v in _L0_xattn_all.items() if k in ('Wk', 'bk', 'Wq', 'bq', 'Wv', 'bv', 'Wck', 'bck', 'Wcq', 'bcq', 'Wcv', 'bcv', 'Wp', 'bp')}
    del _L0_xattn_all

    def _L0_ffn_setup():
        import jax, jax.numpy as jnp
        import numpy as np
        D_MODEL, D_FF, RANK = (256, 1024, 64)
        B, S = (4, 1024)
        key = jax.random.key(seed)
        ks = jax.random.split(key, 7)
        return {'x': jax.random.normal(ks[0], (B, S, D_MODEL), dtype=jnp.float32), 'U1': jax.random.normal(ks[1], (D_MODEL, RANK), dtype=jnp.float32) * 0.02, 'V1': jax.random.normal(ks[2], (RANK, D_FF), dtype=jnp.float32) * 0.02, 'b1': jnp.zeros((D_FF,), dtype=jnp.float32), 'U2': jax.random.normal(ks[3], (D_FF, RANK), dtype=jnp.float32) * 0.02, 'V2': jax.random.normal(ks[4], (RANK, D_MODEL), dtype=jnp.float32) * 0.02, 'b2': jnp.zeros((D_MODEL,), dtype=jnp.float32)}
    _L0_ffn_all = _L0_ffn_setup()
    _L0_ffn_in = {k: v for k, v in _L0_ffn_all.items() if k in ('U1', 'V1', 'b1', 'U2', 'V2', 'b2')}
    del _L0_ffn_all
    return {'x': x, 'ctx_512': ctx_512, 'L0_attn_pre_norm_w': _L0_attn_in['pre_norm_w'], 'L0_attn_in_proj_w': _L0_attn_in['in_proj_w'], 'L0_attn_short_w': _L0_attn_in['short_w'], 'L0_attn_short_b': _L0_attn_in['short_b'], 'L0_attn_log_poles': _L0_attn_in['log_poles'], 'L0_attn_residues': _L0_attn_in['residues'], 'L0_attn_D_skip': _L0_attn_in['D_skip'], 'L0_attn_out_proj_w': _L0_attn_in['out_proj_w'], 'L0_attn_post_norm_w': _L0_attn_in['post_norm_w'], 'L0_attn_l1_w': _L0_attn_in['l1_w'], 'L0_attn_l2_w': _L0_attn_in['l2_w'], 'L0_attn_l3_w': _L0_attn_in['l3_w'], 'L0_xattn_Wk': _L0_xattn_in['Wk'], 'L0_xattn_bk': _L0_xattn_in['bk'], 'L0_xattn_Wq': _L0_xattn_in['Wq'], 'L0_xattn_bq': _L0_xattn_in['bq'], 'L0_xattn_Wv': _L0_xattn_in['Wv'], 'L0_xattn_bv': _L0_xattn_in['bv'], 'L0_xattn_Wck': _L0_xattn_in['Wck'], 'L0_xattn_bck': _L0_xattn_in['bck'], 'L0_xattn_Wcq': _L0_xattn_in['Wcq'], 'L0_xattn_bcq': _L0_xattn_in['bcq'], 'L0_xattn_Wcv': _L0_xattn_in['Wcv'], 'L0_xattn_bcv': _L0_xattn_in['bcv'], 'L0_xattn_Wp': _L0_xattn_in['Wp'], 'L0_xattn_bp': _L0_xattn_in['bp'], 'L0_ffn_U1': _L0_ffn_in['U1'], 'L0_ffn_V1': _L0_ffn_in['V1'], 'L0_ffn_b1': _L0_ffn_in['b1'], 'L0_ffn_U2': _L0_ffn_in['U2'], 'L0_ffn_V2': _L0_ffn_in['V2'], 'L0_ffn_b2': _L0_ffn_in['b2']}

def reference(x, ctx_512, L0_attn_pre_norm_w, L0_attn_in_proj_w, L0_attn_short_w, L0_attn_short_b, L0_attn_log_poles, L0_attn_residues, L0_attn_D_skip, L0_attn_out_proj_w, L0_attn_post_norm_w, L0_attn_l1_w, L0_attn_l2_w, L0_attn_l3_w, L0_xattn_Wk, L0_xattn_bk, L0_xattn_Wq, L0_xattn_bq, L0_xattn_Wv, L0_xattn_bv, L0_xattn_Wck, L0_xattn_bck, L0_xattn_Wcq, L0_xattn_bcq, L0_xattn_Wcv, L0_xattn_bcv, L0_xattn_Wp, L0_xattn_bp, L0_ffn_U1, L0_ffn_V1, L0_ffn_b1, L0_ffn_U2, L0_ffn_V2, L0_ffn_b2):
    import jax
    import jax.numpy as jnp

    def _L0_attn_ref(u, pre_norm_w, in_proj_w, short_w, short_b, log_poles, residues, D_skip, out_proj_w, post_norm_w, l1_w, l2_w, l3_w):
        import jax, jax.numpy as jnp
        import numpy as np
        B, L, D, S, K, FF = (2, 1024, 256, 16, 3, 672)
        EPS = 1e-06

        def rmsnorm(x, w):
            var = jnp.mean(x * x, axis=-1, keepdims=True)
            return x * jax.lax.rsqrt(var + EPS) * w
        Lc = u.shape[1]
        z = rmsnorm(u, pre_norm_w) @ in_proj_w.T
        zc = z.transpose(0, 2, 1)
        z_pre = jax.lax.conv_general_dilated(zc, short_w, window_strides=(1,), padding=[(K - 1, 0)], dimension_numbers=('NCH', 'OIH', 'NCH'), feature_group_count=3 * D)
        z_pre = z_pre + short_b[None, :, None]
        x2, x1, v = jnp.split(z_pre, 3, axis=1)
        t = jnp.arange(Lc, dtype=jnp.float32)
        h = jnp.sum(residues[:, :, None] * jnp.exp(log_poles * t[None, None, :]), axis=1)
        xv = x1 * v
        n = 2 * Lc
        Xf = jnp.fft.rfft(xv, n=n)
        Hf = jnp.fft.rfft(h, n=n)
        yconv = jnp.fft.irfft(Xf * Hf[None], n=n)[..., :Lc]
        y = (yconv + xv * D_skip[None, :, None]) * x2
        y = y.transpose(0, 2, 1)
        y = y @ out_proj_w.T + u
        zm = rmsnorm(y, post_norm_w)
        mlp = jax.nn.gelu(zm @ l1_w.T) * (zm @ l2_w.T) @ l3_w.T
        return y + mlp

    def _L0_xattn_ref(x, cross_input, Wk, bk, Wq, bq, Wv, bv, Wck, bck, Wcq, bcq, Wcv, bcv, Wp, bp):
        import jax, jax.numpy as jnp
        import numpy as np
        B, T, TC, C, CC, H = (2, 512, 128, 256, 128, 16)
        D = C // H

        def _heads(t):
            b, l, _ = t.shape
            return t.reshape(b, l, H, D).transpose(0, 2, 1, 3)
        scale = np.float32(1.0 / np.sqrt(D))
        q = _heads(x @ Wq + bq)
        k = _heads(x @ Wk + bk)
        v = _heads(x @ Wv + bv)
        att = jnp.einsum('bhqd,bhkd->bhqk', q, k) * scale
        causal = jnp.tril(jnp.ones((T, T), bool))
        att = jnp.where(causal[None, None], att, -jnp.inf)
        y = jnp.einsum('bhqk,bhkd->bhqd', jax.nn.softmax(att, axis=-1), v)
        qc = _heads(x @ Wcq + bcq)
        kc = _heads(cross_input @ Wck + bck)
        vc = _heads(cross_input @ Wcv + bcv)
        attc = jnp.einsum('bhqd,bhkd->bhqk', qc, kc) * scale
        y = y + jnp.einsum('bhqk,bhkd->bhqd', jax.nn.softmax(attc, axis=-1), vc)
        y = y.transpose(0, 2, 1, 3).reshape(x.shape[0], T, C)
        return y @ Wp + bp

    def _L0_ffn_ref(x, U1, V1, b1, U2, V2, b2):
        import jax, jax.numpy as jnp
        import numpy as np
        D_MODEL, D_FF, RANK = (256, 1024, 64)
        B, S = (4, 1024)
        P = jnp.einsum('bsd,dr->bsr', x, U1)
        H = jax.nn.gelu(jnp.einsum('bsr,rf->bsf', P, V1) + b1)
        Q = jnp.einsum('bsf,fr->bsr', H, U2)
        return jnp.einsum('bsr,rd->bsd', Q, V2) + b2
    x = _layernorm(x + _L0_attn_ref(x, L0_attn_pre_norm_w, L0_attn_in_proj_w, L0_attn_short_w, L0_attn_short_b, L0_attn_log_poles, L0_attn_residues, L0_attn_D_skip, L0_attn_out_proj_w, L0_attn_post_norm_w, L0_attn_l1_w, L0_attn_l2_w, L0_attn_l3_w), axis=-1)
    x = _layernorm(x + _L0_xattn_ref(x, ctx_512, L0_xattn_Wk, L0_xattn_bk, L0_xattn_Wq, L0_xattn_bq, L0_xattn_Wv, L0_xattn_bv, L0_xattn_Wck, L0_xattn_bck, L0_xattn_Wcq, L0_xattn_bcq, L0_xattn_Wcv, L0_xattn_bcv, L0_xattn_Wp, L0_xattn_bp), axis=-1)
    x = _layernorm(x + _L0_ffn_ref(x, L0_ffn_U1, L0_ffn_V1, L0_ffn_b1, L0_ffn_U2, L0_ffn_V2, L0_ffn_b2), axis=-1)
    return x

_drawn_inputs = setup_inputs


def setup_inputs(seed=0):
    import zlib

    import numpy as np

    out = dict(_drawn_inputs(seed))
    spreads = {'L0_attn_pre_norm_w': (1.0, 0.2),
     'L0_attn_post_norm_w': (1.0, 0.2),
     'L0_xattn_bk': (0.0, 2.0),
     'L0_xattn_bq': (0.0, 0.645),
     'L0_xattn_bv': (0.0, 0.1),
     'L0_xattn_bck': (0.0, 2.0),
     'L0_xattn_bcq': (0.0, 0.36),
     'L0_xattn_bcv': (0.0, 0.1),
     'L0_xattn_bp': (0.0, 0.1),
     'L0_ffn_b1': (0.0, 0.8),
     'L0_ffn_b2': (0.0, 0.8)}
    factors = {'L0_attn_short_b': 3.367,
     'L0_attn_D_skip': 31.534,
     'L0_ffn_U1': 8.0,
     'L0_ffn_V1': 8.0,
     'L0_ffn_U2': 8.0,
     'L0_ffn_V2': 8.0}
    for name, (base, spread) in spreads.items():
        noise = np.random.default_rng([zlib.crc32(name.encode()), seed]).standard_normal(out[name].shape)
        drawn = base * np.exp(spread * noise) if base else spread * noise
        out[name] = jnp.asarray(drawn.astype(out[name].dtype))
    for name, factor in factors.items():
        out[name] = (out[name] * factor).astype(out[name].dtype)
    return out
```

```python
from contextlib import ExitStack

import concourse.bass as bass
from concourse import mybir

F32 = mybir.dt.float32
F32R = mybir.dt.float32r
BF16 = mybir.dt.bfloat16
ALU = mybir.AluOpType
ACT = mybir.ActivationFunctionType
AX_X = mybir.AxisListType.X

P = 128
B, T, D = 16, 512, 256
KT = D // P
QT = T // P
S = 16
C = 32
NC = T // C
G = D // 4
FF, FT, FM = 672, 6, 112
RMS_EPS, LN_EPS = 1e-6, 1e-5


def wait(eng, sem, value):
    if not isinstance(value, int) or value > 0:
        eng.wait_ge(sem, value)


def over(eng, count, step):
    for n in (0, 1):
        step(n, n)
    with eng.Fori(1, count // 2 - 1, 1) as pair:
        step(2 * pair, 0)
        step(2 * pair + 1, 1)
    for n in (count - 2, count - 1):
        step(n, n % 2)


def is_last(n, count=None):
    return isinstance(n, int) and n == (count or B) - 1


def loads(b, par):
    return 8 * (b - par) + 16


class Names:

    def __init__(self, nc, ctx, tag):
        self.nc, self.ctx, self.tag, self.semaphores = nc, ctx, tag, []

    def sb(self, name, shape, dt=F32):
        return self.ctx.enter_context(self.nc.sbuf_tensor(f"{self.tag}_{name}", shape, dt))

    def psum(self, name, shape, dt=F32):
        return self.ctx.enter_context(self.nc.psum_tensor(f"{self.tag}_{name}", shape, dt))

    def sem(self, name):
        self.semaphores.append(self.ctx.enter_context(self.nc.semaphore(f"{self.tag}_{name}")))
        return self.semaphores[-1]

    def clear(self):
        with self.nc.Block() as block:
            @block.sync
            def _(sp):
                for semaphore in self.semaphores:
                    sp.sem_clear(semaphore)


def group(xv_all, g):
    return xv_all[:, :, bass.ds(g, 1), :].rearrange("p b o n -> p b (o n)")


def settle(eng, settled):
    eng.sem_inc(settled, 1)


def products3(pe, out, left, right, first=True, last=True):
    n = len(left)
    for k, ((lh, ll), (rh, rl)) in enumerate(zip(left, right)):
        pe.matmul(out, lh, rh, start=first and k == 0, stop=False)
        pe.matmul(out, ll, rh, start=False, stop=False)
        mm = pe.matmul(out, lh, rl, start=False, stop=last and k == n - 1)
    return mm


def project(nc, x, w_in, w_scale, taps, tap_bias, c_ident, xv_all, x2_d):
    CT = 3 * KT
    ORDER = [2, 4, 3, 5, 0, 1]
    with ExitStack() as ctx:
        n = Names(nc, ctx, "pj")
        ident = n.sb("ident", [P, P])
        w_raw = n.sb("w_raw", [P, KT, 3 * D])
        w_hi = n.sb("w_hi", [P, KT, 3 * D], F32R)
        w_lo = n.sb("w_lo", [P, KT, 3 * D], F32R)
        wsc = n.sb("wsc", [P, KT])
        tap = n.sb("tap", [P, CT, 3])
        tb = n.sb("tb", [P, CT])
        xin = [n.sb(f"xin{i}", [P, QT, D]) for i in range(2)]
        xn = [n.sb(f"xn{i}", [P, QT, D]) for i in range(2)]
        ss = [n.sb(f"ss{i}", [P, QT]) for i in range(2)]
        ms = [n.sb(f"ms{i}", [P, QT]) for i in range(2)]
        rstd = [n.sb(f"rstd{i}", [P, QT]) for i in range(2)]
        mhalf = n.sb("mhalf", [P, QT])
        x_hi = [n.sb(f"x_hi{i}", [P, KT, T], F32R) for i in range(2)]
        x_lo = [n.sb(f"x_lo{i}", [P, KT, T], F32R) for i in range(2)]
        zc = [n.sb(f"zc{i}", [P, CT, T]) for i in range(2)]
        xv = [n.sb(f"xv{i}", [P, KT, T]) for i in range(1)] * 2
        turned_xv = [n.sb(f"turned_xv{i}", [P, G, NC]) for i in range(2)]
        ps_t = n.psum("ps_t", [P, KT, T])
        ps_z = [n.psum(f"ps_z{i}", [P, T]) for i in range(CT)]

        par_loaded, w_loaded, w_scaled, w_high, w_split = (n.sem(s) for s in ("par_loaded", "w_loaded", "w_scaled", "w_high", "w_split"))
        x_loaded = [n.sem(f"x_loaded{i}") for i in range(2)]
        x2_stored = [n.sem(f"x2_stored{i}") for i in range(2)]
        placed = [n.sem(f"placed{i}") for i in range(2)]
        const_set, squared, ms_set, rstd_set, normed, turned, high_set, low_set = (
            n.sem(s) for s in ("const_set", "squared", "ms_set", "rstd_set", "normed", "turned", "high_set", "low_set"))
        z_ready, tap2_done, tap1_done, tap0_done, gated, chunked = (
            n.sem(s) for s in ("z_ready", "tap2_done", "tap1_done", "tap0_done", "gated", "chunked"))
        pool_settled = n.sem("pool_settled")
        ctx.callback(n.clear)
        block = ctx.enter_context(nc.Block())

        @block.sync
        def _(sp):
            sp.dma_start(w_raw[:], w_in).then_inc(w_loaded, 16)
            sp.dma_start(ident[:], c_ident).then_inc(par_loaded, 16)
            sp.dma_start(wsc[:], w_scale).then_inc(par_loaded, 16)
            sp.dma_start(tap[:], taps).then_inc(par_loaded, 16)
            sp.dma_start(tb[:], tap_bias).then_inc(par_loaded, 16)

            def load(b, par):
                wait(sp, normed, QT * (b - 1))
                sp.dma_start(xin[par][:],
                             x[bass.ds(b, 1)].rearrange("o (q p) d -> p (o q) d", p=P)).then_inc(x_loaded[par], 16)

            def store(b, par):
                sp.wait_ge(tap0_done, CT * (b + 1))
                sp.dma_start(x2_d[bass.ds(b, 1)].rearrange("o p k t -> (o p) k t"),
                             zc[par][:, 0:KT, :]).then_inc(x2_stored[par], 16)
                sp.wait_ge(chunked, KT * (b + 1))
                sp.dma_start(xv_all[:, bass.ds(b, 1)].rearrange("p o g n -> p (o g n)"),
                             turned_xv[par][:].rearrange("p g n -> p (g n)")).then_inc(placed[par], 16)

            load(0, 0)
            load(1, 1)

            def step(b, par):
                if not isinstance(b, int) or b + 2 < B:
                    load(b + 2, par)
                store(b, par)
            over(sp, B, step)
            for i in range(2):
                sp.wait_ge(x2_stored[i], 16 * (B // 2))
                sp.wait_ge(placed[i], 16 * (B // 2))

        @block.scalar
        def _(act):
            def squares(b, par):
                act.wait_ge(x_loaded[par], loads(b, par))
                wait(act, turned, b - 1)
                for q in range(QT):
                    act.activation(xn[par][:, q, :], xin[par][:, q, :], ACT.Square,
                                   accum_out=ss[par][:, q:q + 1]).then_inc(squared, 1)

            def high(b, par):
                act.wait_ge(turned, b + 1)
                wait(act, z_ready, CT * (b - 1))
                act.activation(x_hi[par][:], ps_t[:], ACT.Copy).then_inc(high_set, 1)

            squares(0, 0)
            high(0, 0)
            act.wait_ge(par_loaded, 64)

            def step(b, par):
                last = is_last(b)
                if not last:
                    squares(b + 1, 1 - par)
                for k, ct in enumerate(ORDER):
                    act.wait_ge(z_ready, CT * b + k + 1)
                    if ct < KT:
                        wait(act, x2_stored[par], loads(b, par) - 16)
                    else:
                        wait(act, gated, KT * (b - 1))
                    act.activation(zc[par][:, ct, :], ps_z[ct][:], ACT.Identity, bias=tb[:, ct:ct + 1],
                                   scale=tap[:, ct, 2:3]).then_inc(tap2_done, 1)
                    if k == 3 and not last:
                        high(b + 1, 1 - par)
            over(act, B, step)

        @block.gpsimd
        def _(pool):
            pool.memset(mhalf[:], -0.5).then_inc(const_set, 1)
            pool.wait_ge(const_set, 1)

            def root(b, par):
                pool.wait_ge(squared, QT * (b + 1))
                settle(pool, pool_settled)
                pool.tensor_scalar(ms[par][:], ss[par][:], 1.0 / D, RMS_EPS, ALU.mult, ALU.add).then_inc(ms_set, 1)
                pool.wait_ge(ms_set, b + 1)
                wait(pool, normed, QT * (b - 1))
                pool.tensor_tensor(rstd[par][:], ms[par][:], mhalf[:], ALU.pow).then_inc(rstd_set, 1)

            root(0, 0)

            def step(b, par):
                if not is_last(b):
                    root(b + 1, 1 - par)
                for k in range(KT):
                    pool.wait_ge(tap0_done, CT * b + 2 * k + 2)
                    wait(pool, chunked, KT * (b - 1) + k + 1)
                    pool.tensor_tensor(xv[par][:, k, :], zc[par][:, KT + k, :], zc[par][:, 2 * KT + k, :],
                                       ALU.mult).then_inc(gated, 1)
            over(pool, B, step)

        @block.tensor
        def _(pe):
            pe.wait_ge(par_loaded, 64)

            def turn(b, par):
                pe.wait_ge(normed, QT * (b + 1))
                wait(pe, low_set, b)
                for k in range(KT):
                    for q in range(QT):
                        mm = pe.transpose(ps_t[:, k, q * P:(q + 1) * P], xn[par][:, q, k * P:(k + 1) * P], ident[:])
                mm.then_inc(turned, 1)

            turn(0, 0)
            pe.wait_ge(w_split, 1)

            def step(b, par):
                pe.wait_ge(low_set, b + 1)
                for k, ct in enumerate(ORDER):
                    wait(pe, tap0_done, CT * (b - 1) + k + 1)
                    cols = slice(ct * P, (ct + 1) * P)
                    products3(pe, ps_z[ct][:], [(w_hi[:, j, cols], w_lo[:, j, cols]) for j in range(KT)],
                              [(x_hi[par][:, j, :], x_lo[par][:, j, :]) for j in range(KT)]).then_inc(z_ready, 1)
                    if k == 2 and not is_last(b):
                        turn(b + 1, 1 - par)
            over(pe, B, step)

        @block.vector
        def _(dve):
            def norm(b, par):
                dve.wait_ge(rstd_set, b + 1)
                for q in range(QT):
                    dve.tensor_scalar(xn[par][:, q, :], xin[par][:, q, :], rstd[par][:, q:q + 1], None,
                                      ALU.mult).then_inc(normed, 1)

            def low(b, par):
                dve.wait_ge(high_set, b + 1)
                dve.tensor_tensor(x_lo[par][:], ps_t[:], x_hi[par][:].bitcast(F32), ALU.subtract).then_inc(low_set, 1)

            dve.wait_ge(w_loaded, 16)
            dve.wait_ge(par_loaded, 64)
            for k in range(KT):
                dve.tensor_scalar(w_raw[:, k, :], w_raw[:, k, :], wsc[:, k:k + 1], None, ALU.mult).then_inc(w_scaled, 1)
            dve.wait_ge(w_scaled, KT)
            dve.tensor_copy(w_hi[:], w_raw[:]).then_inc(w_high, 1)
            dve.wait_ge(w_high, 1)
            dve.tensor_tensor(w_lo[:], w_raw[:], w_hi[:].bitcast(F32), ALU.subtract).then_inc(w_split, 1)
            norm(0, 0)
            low(0, 0)

            def step(b, par):
                last = is_last(b)
                if not last:
                    norm(b + 1, 1 - par)

                def chunk(k):
                    if k == 0:
                        wait(dve, placed[par], loads(b, par) - 16)
                    dve.wait_ge(gated, KT * b + k + 1)
                    dst = turned_xv[par][:, k * C:(k + 1) * C, :].rearrange("p c n -> p n c")
                    dve.transpose(dst, xv[par][:, k, :].rearrange("p (n c) -> p n c", c=C)).then_inc(chunked, 1)

                for k, ct in enumerate(ORDER):
                    dve.wait_ge(tap2_done, CT * b + k + 1)
                    dve.scalar_tensor_tensor(zc[par][:, ct, 1:T], ps_z[ct][:, 0:T - 1], tap[:, ct, 1:2],
                                             zc[par][:, ct, 1:T], ALU.mult, ALU.add).then_inc(tap1_done, 1)
                    dve.wait_ge(tap1_done, CT * b + k + 1)
                    dve.scalar_tensor_tensor(zc[par][:, ct, 2:T], ps_z[ct][:, 0:T - 2], tap[:, ct, 0:1],
                                             zc[par][:, ct, 2:T], ALU.mult, ALU.add).then_inc(tap0_done, 1)
                    if k == 3 and not last:
                        low(b + 1, 1 - par)
                    if k >= 4:
                        chunk(k - 4)
            over(dve, B, step)


def longconv(nc, lp_rows, lp_cols, res_cols, lp_chan, res_chan, skip, c_left, c_ramp, c_lag, c_qmask, c_gmask,
             c_notfirst, filt_d, xv_all):
    NP = G // 2
    W = B * NC
    with ExitStack() as ctx:
        n = Names(nc, ctx, "lc")
        lr = n.sb("lr", [P, G, S])
        to_end = n.sb("to_end", [P, G, S])
        left = n.sb("left", [P, 1])
        lc = n.sb("lc", [P, NP])
        rc = n.sb("rc", [P, NP])
        ramp = n.sb("ramp", [P, C])
        readout = n.sb("readout", [P, NP, C])
        lam = n.sb("lam", [P, NP])
        lch = n.sb("lch", [P, KT, S])
        rch = n.sb("rch", [P, KT, S])
        dsk = n.sb("dsk", [P, KT])
        lag = n.sb("lag", [P, C])
        hexp = n.sb("hexp", [P, KT, C, S])
        h = n.sb("h", [P, KT, 2 * C])
        toep = n.sb("toep", [P, G, C])
        qmask = n.sb("qmask", [P, 4])
        gmask = n.sb("gmask", [P, 2, 4])
        notfirst = n.sb("notfirst", [P, W])
        enter = [[n.sb(f"enter{i}{g}", [P, 4, 2, S]) for g in range(2)] for i in range(2)]
        inside = [n.sb(f"inside{i}", [P, 2, 4, C]) for i in range(2)]
        leave = [n.sb(f"leave{i}", [P, 2, 4, C]) for i in range(2)]
        carry = [n.sb(f"carry{i}", [P, W]) for i in range(2)]
        state = [n.sb(f"state{i}", [P, W + 1]) for i in range(2)]
        ps_u = [n.psum(f"ps_u{i}", [P, 512]) for i in range(2)]
        ps_y = [[n.psum(f"ps_y{i}{g}", [P, 512]) for g in range(2)] for i in range(2)]
        loaded, filt_out, filt_in, zeroed = (n.sem(s) for s in ("loaded", "filt_out", "filt_in", "zeroed"))
        exp_in, exp_out, filt_done, read_done = (n.sem(s) for s in ("exp_in", "exp_out", "filt_done", "read_done"))
        built, carry_set, gathered, scanned, restarted, summed, stored = (
            n.sem(s) for s in ("built", "carry_set", "gathered", "scanned", "restarted", "summed", "stored"))
        block = ctx.enter_context(nc.Block())
        LOADS = 4 + 11

        @block.sync
        def _(sp):
            for q in range(4):
                sp.dma_start(lr[q * C:(q + 1) * C].rearrange("p g s -> p (g s)"),
                             bass.AP(lp_rows.tensor, q * G * S, [[0, C], [1, G * S]])).then_inc(loaded, 16)
            for dst, src in ((lc, lp_cols), (rc, res_cols), (lch, lp_chan), (rch, res_chan), (dsk, skip), (left, c_left),
                             (ramp, c_ramp), (lag, c_lag), (qmask, c_qmask), (gmask, c_gmask), (notfirst, c_notfirst)):
                sp.dma_start(dst[:], src).then_inc(loaded, 16)
            sp.wait_ge(filt_done, 3 * KT + 1)
            for k in range(KT):
                sp.dma_start(bass.AP(filt_d.tensor, k * C * 2 * C, [[G * 2 * C, 4], [2 * C, C], [1, 2 * C]]),
                             h[:, k, :]).then_inc(filt_out, 16)
            sp.wait_ge(filt_out, 16 * KT)
            for j in range(C):
                sp.dma_start(toep[j::C], bass.AP(filt_d.tensor, C - j, [[G * 2 * C, 4], [2 * C, G], [1, C]])).then_inc(filt_in, 16)

        @block.scalar
        def _(act):
            act.wait_ge(loaded, 16 * LOADS)
            act.activation(to_end[:], lr[:], ACT.Exp, scale=left[:, 0:1]).then_inc(exp_out, 1)
            act.activation(lam[:], lc[:], ACT.Exp, scale=float(C)).then_inc(exp_out, 1)
            for k in range(KT):
                act.wait_ge(exp_in, k + 1)
                act.activation(hexp[:, k], hexp[:, k], ACT.Exp).then_inc(exp_out, 1)
            act.wait_ge(exp_in, KT + 1)
            act.activation(readout[:], readout[:], ACT.Exp).then_inc(exp_out, 1)

            def step(p, par):
                act.wait_ge(summed, 2 * p + 2)
                for g in range(2):
                    act.activation(group(xv_all, 2 * p + g),
                                   ps_y[par][g][:, 0:W].rearrange("p (b n) -> p b n", n=NC), ACT.Copy).then_inc(stored, 1)
            over(act, NP, step)

        @block.gpsimd
        def _(pool):
            for i in range(2):
                for g in range(2):
                    pool.memset(enter[i][g][:], 0.0).then_inc(zeroed, 1)
            pool.wait_ge(zeroed, 4)
            pool.wait_ge(loaded, 16 * LOADS)
            pool.wait_ge(exp_out, 1)
            pool.wait_ge(read_done, 1)
            pool.wait_ge(filt_in, 16 * C)

            def step(p, par):
                wait(pool, summed, 2 * (p - 1))
                for g in range(2):
                    pool.tensor_tensor(enter[par][g][:, :, g, :],
                                       to_end[:, bass.ds(2 * p + g, 1), :].to_broadcast([P, 4, S]),
                                       qmask[:].unsqueeze(2).to_broadcast([P, 4, S]), ALU.mult).then_inc(built, 1)
                pool.tensor_tensor(inside[par][:],
                                   toep[:, bass.ds(2 * p, 2), :].unsqueeze(2).to_broadcast([P, 2, 4, C]),
                                   qmask[:].unsqueeze(1).unsqueeze(3).to_broadcast([P, 2, 4, C]), ALU.mult).then_inc(built, 1)
                pool.tensor_tensor(leave[par][:].rearrange("p g q i -> p (g q) i"),
                                   readout[:, bass.ds(p, 1), :].to_broadcast([P, 8, C]),
                                   gmask[:].rearrange("p g q -> p (g q)").unsqueeze(2).to_broadcast([P, 8, C]),
                                   ALU.mult).then_inc(built, 1)
            over(pool, NP, step)

        @block.tensor
        def _(pe):
            def gather(p, par):
                pe.wait_ge(built, 4 * (p + 1))
                wait(pe, scanned, p - 1)
                for g in range(2):
                    mm = pe.matmul(ps_u[par][:, 0:W].rearrange("p (b n) -> p b n", n=NC), enter[par][g][:].rearrange("p q g s -> p (q g s)"),
                                   group(xv_all, 2 * p + g), start=g == 0, stop=g == 1)
                mm.then_inc(gathered, 1)

            gather(0, 0)

            def step(p, par):
                if not is_last(p, NP):
                    gather(p + 1, 1 - par)
                wait(pe, stored, 2 * (p - 1))
                pe.wait_ge(restarted, p + 1)
                for g in range(2):
                    pe.matmul(ps_y[par][g][:, 0:W].rearrange("p (b n) -> p b n", n=NC), inside[par][:, g].rearrange("p q i -> p (q i)"),
                              group(xv_all, 2 * p + g), start=True, stop=False)
                    pe.matmul(ps_y[par][g][:, 0:W], leave[par][:, g].rearrange("p q i -> p (q i)"),
                              state[par][:, 0:W], start=False, stop=True).then_inc(summed, 1)
            over(pe, NP, step)

        @block.vector
        def _(dve):
            dve.memset(h[:], 0.0).then_inc(filt_done, 1)
            dve.wait_ge(loaded, 16 * LOADS)
            for k in range(KT):
                dve.tensor_tensor(hexp[:, k], lch[:, k].unsqueeze(1).to_broadcast([P, C, S]),
                                  lag[:].unsqueeze(2).to_broadcast([P, C, S]), ALU.mult).then_inc(exp_in, 1)
            dve.tensor_tensor(readout[:], lc[:].unsqueeze(2).to_broadcast([P, NP, C]),
                              ramp[:].unsqueeze(1).to_broadcast([P, NP, C]), ALU.mult).then_inc(exp_in, 1)
            dve.wait_ge(filt_done, 1)
            for k in range(KT):
                dve.wait_ge(exp_out, 3 + k)
                dve.tensor_tensor(hexp[:, k], hexp[:, k], rch[:, k].unsqueeze(1).to_broadcast([P, C, S]),
                                  ALU.mult).then_inc(filt_done, 1)
                dve.wait_ge(filt_done, 3 * k + 2)
                dve.tensor_reduce(h[:, k, C:2 * C], hexp[:, k], AX_X, ALU.add).then_inc(filt_done, 1)
                dve.wait_ge(filt_done, 3 * k + 3)
                dve.tensor_tensor(h[:, k, C:C + 1], h[:, k, C:C + 1], dsk[:, k:k + 1], ALU.add).then_inc(filt_done, 1)
            dve.wait_ge(exp_out, 5)
            dve.tensor_tensor(readout[:], readout[:], rc[:].unsqueeze(2).to_broadcast([P, NP, C]), ALU.mult).then_inc(read_done, 1)

            def step(p, par):
                wait(dve, scanned, p - 1)
                dve.tensor_scalar(carry[par][:], notfirst[:], lam[:, bass.ds(p, 1)], None, ALU.mult).then_inc(carry_set, 1)
                dve.wait_ge(carry_set, p + 1)
                dve.wait_ge(gathered, p + 1)
                wait(dve, summed, 2 * (p - 1))
                dve.tensor_tensor_scan(state[par][:, 1:W + 1], carry[par][:], ps_u[par][:, 0:W], 0.0,
                                       ALU.mult, ALU.add).then_inc(scanned, 1)
                dve.wait_ge(scanned, p + 1)
                dve.memset(state[par][:, 0:W].rearrange("p (b c) -> p b c", c=NC)[:, :, 0:1], 0.0).then_inc(restarted, 1)
            over(dve, NP, step)
def mlp(nc, x, x2_d, w_out, w_gate, w_up, w_down, w_scale, c_ident, xv_all, x1_d):
    with ExitStack() as ctx:
        n = Names(nc, ctx, "ml")
        ident = n.sb("ident", [P, P])
        wsc = n.sb("wsc", [P, KT])
        raw = n.sb("raw", [P, FT * D])
        wo = [n.sb(f"wo{i}", [P, KT, D], F32R) for i in range(2)]
        wg = [n.sb(f"wg{i}", [P, KT, FF], F32R) for i in range(2)]
        wu = [n.sb(f"wu{i}", [P, KT, FF], F32R) for i in range(2)]
        wd = [n.sb(f"wd{i}", [FM, FT, D], F32R) for i in range(2)]
        x2 = n.sb("x2", [P, KT, T])
        xin = n.sb("xin", [P, QT, D])
        turned_y = n.sb("turned_y", [P, G, NC])
        y2 = n.sb("y2", [P, KT, T])
        y2_hi = n.sb("y2_hi", [P, KT, T], F32R)
        y2_lo = n.sb("y2_lo", [P, KT, T], F32R)
        y1 = n.sb("y1", [P, QT, D])
        yn = n.sb("yn", [P, QT, D])
        xy = [n.sb(f"xy{i}", [P, QT, D]) for i in range(2)]
        t_hi = [n.sb(f"t_hi{i}", [P, KT, T], F32R) for i in range(2)]
        t_lo = [n.sb(f"t_lo{i}", [P, KT, T], F32R) for i in range(2)]
        gl = [n.sb(f"gl{i}", [FM, T]) for i in range(2)]
        m = [n.sb(f"m{i}", [FM, T]) for i in range(2)]
        m_hi = [n.sb(f"m_hi{i}", [FM, T], F32R) for i in range(FT + 2)]
        m_lo = [n.sb(f"m_lo{i}", [FM, T], F32R) for i in range(FT + 2)]
        r = n.sb("r", [P, QT, D])
        ss, ms, rstd, mhalf, lnv, lnr = (n.sb(s, [P, QT]) for s in ("ss", "ms", "rstd", "mhalf", "lnv", "lnr"))
        bn, mv = n.sb("bn", [P, QT, 6]), n.sb("mv", [P, QT, 2])
        ps_o = n.psum("ps_o", [P, QT, D])
        ps_t = n.psum("ps_t", [P, KT, T])
        ps_g = [n.psum(f"ps_g{i}", [P, T]) for i in range(2)]
        ps_u = [n.psum(f"ps_u{i}", [P, T]) for i in range(2)]
        par_loaded, w_loaded, w_scaled, w_high, w_low, const_set = (
            n.sem(s) for s in ("par_loaded", "w_loaded", "w_scaled", "w_high", "w_low", "const_set"))
        x2_loaded, x_loaded, x1_stored, y_fetched = (n.sem(s) for s in ("x2_loaded", "x_loaded", "x1_stored", "y_fetched"))
        unchunked, gated, y2_high, y2_low, out_ready, y1_set = (
            n.sem(s) for s in ("unchunked", "gated", "y2_high", "y2_low", "out_ready", "y1_set"))
        squared, ms_set, rstd_set, normed, turned, high_set, low_set, xy_set = (
            n.sem(s) for s in ("squared", "ms_set", "rstd_set", "normed", "turned", "high_set", "low_set", "xy_set"))
        fed, gelu_done, prod_done, m_high, m_low, down_ready = (
            n.sem(s) for s in ("fed", "gelu_done", "prod_done", "m_high", "m_low", "down_ready"))
        r_set, stats, aggr, lnv_set, lnr_set, x1_set = (
            n.sem(s) for s in ("r_set", "stats", "aggr", "lnv_set", "lnr_set", "x1_set"))
        pool_settled, dve_settled = n.sem("pool_settled"), n.sem("dve_settled")
        block = ctx.enter_context(nc.Block())

        def slot(k, par):
            return 2 * par + k if k < 2 else k + 2

        raws = [(w_out, KT * D), (w_gate, KT * FF), (w_up, KT * FF), (w_down, FT * D)]

        @block.sync
        def _(sp):
            sp.dma_start(ident[:], c_ident).then_inc(par_loaded, 16)
            sp.dma_start(wsc[:], w_scale).then_inc(par_loaded, 16)
            for k, (w, size) in enumerate(raws):
                wait(sp, w_low, k)
                rows = FM if k == 3 else P
                sp.dma_start(raw[0:rows, 0:size], w.rearrange("p k m -> p (k m)")).then_inc(w_loaded, 16)

            def load_x2(b):
                wait(sp, unchunked, KT * b)
                sp.dma_start(turned_y[:].rearrange("p g n -> p (g n)"),
                             xv_all[:, bass.ds(b, 1)].rearrange("p o g n -> p (o g n)")).then_inc(y_fetched, 16)
                wait(sp, gated, b)
                sp.dma_start(x2[:], x2_d[bass.ds(b, 1)].rearrange("o p k t -> (o p) k t")).then_inc(x2_loaded, 16)

            def load_x(b):
                wait(sp, xy_set, b)
                sp.dma_start(xin[:], x[bass.ds(b, 1)].rearrange("o (q p) d -> p (o q) d", p=P)).then_inc(x_loaded, 16)

            def store(b):
                sp.wait_ge(x1_set, QT * (b + 1))
                sp.dma_start(x1_d[bass.ds(b, 1)].rearrange("o p q d -> (o p) q d"), r[:]).then_inc(x1_stored, 16)

            load_x2(0)
            load_x(0)
            load_x2(1)
            load_x(1)

            def step(b, par):
                if not (isinstance(b, int) and b + 2 >= B):
                    load_x2(b + 2)
                    load_x(b + 2)
                if not (isinstance(b, int) and b == 0):
                    store(b - 1)
            over(sp, B, step)
            store(B - 1)
            sp.wait_ge(x1_stored, 16 * B)

        @block.scalar
        def _(act):
            def y2_split(b):
                act.wait_ge(gated, b + 1)
                wait(act, out_ready, b)
                act.activation(y2_hi[:], y2[:], ACT.Copy).then_inc(y2_high, 1)

            def squares(b):
                act.wait_ge(y1_set, b + 1)
                wait(act, turned, b)
                for q in range(QT):
                    act.activation(yn[:, q, :], y1[:, q, :], ACT.Square, accum_out=ss[:, q:q + 1]).then_inc(squared, 1)

            def high(b, par):
                act.wait_ge(turned, b + 1)
                wait(act, fed, FT * (b - 1))
                act.activation(t_hi[par][:], ps_t[:], ACT.Copy).then_inc(high_set, 1)

            def product_high(b, par, k):
                act.wait_ge(prod_done, FT * b + k + 1)
                if k >= 2:
                    wait(act, down_ready, b)
                else:
                    wait(act, down_ready, b - 1)
                act.activation(m_hi[slot(k, par)][:], m[k % 2][:], ACT.Copy).then_inc(m_high, 1)

            y2_split(0)
            squares(0)
            high(0, 0)
            y2_split(1)

            def step(b, par):
                for k in range(FT):
                    act.wait_ge(fed, FT * b + k + 1)
                    wait(act, prod_done, FT * b + k - 1)
                    act.activation(gl[k % 2][:], ps_g[k % 2][0:FM, :], ACT.Gelu_apprx_tanh).then_inc(gelu_done, 1)
                    if k >= 1:
                        product_high(b, par, k - 1)
                    if k == 2 and not is_last(b):
                        squares(b + 1)
                    if k == 4 and not is_last(b):
                        high(b + 1, 1 - par)
                product_high(b, par, FT - 1)
                if not (isinstance(b, int) and b + 2 >= B):
                    y2_split(b + 2)
            over(act, B, step)

        @block.gpsimd
        def _(pool):
            pool.memset(mhalf[:], -0.5).then_inc(const_set, 1)
            pool.wait_ge(const_set, 1)

            def y2_rest(b):
                pool.wait_ge(y2_high, b + 1)
                wait(pool, out_ready, b)
                pool.tensor_tensor(y2_lo[:], y2[:], y2_hi[:].bitcast(F32), ALU.subtract).then_inc(y2_low, 1)

            def root(b):
                pool.wait_ge(squared, QT * (b + 1))
                settle(pool, pool_settled)
                pool.tensor_scalar(ms[:], ss[:], 1.0 / D, RMS_EPS, ALU.mult, ALU.add).then_inc(ms_set, 1)
                pool.wait_ge(ms_set, b + 1)
                wait(pool, normed, QT * b)
                pool.tensor_tensor(rstd[:], ms[:], mhalf[:], ALU.pow).then_inc(rstd_set, 1)

            def residual(b, par):
                pool.wait_ge(y1_set, b + 1)
                wait(pool, r_set, b - 1)
                pool.tensor_tensor(xy[par][:], xin[:], y1[:], ALU.add).then_inc(xy_set, 1)

            def ln_root(b):
                pool.wait_ge(aggr, QT * (b + 1))
                settle(pool, pool_settled)
                pool.tensor_scalar(lnv[:], mv[:, :, 1], 1.0, LN_EPS, ALU.mult, ALU.add).then_inc(lnv_set, 1)
                pool.wait_ge(lnv_set, b + 1)
                wait(pool, x1_set, QT * b)
                pool.tensor_tensor(lnr[:], lnv[:], mhalf[:], ALU.pow).then_inc(lnr_set, 1)

            y2_rest(0)
            root(0)
            residual(0, 0)
            y2_rest(1)

            def step(b, par):
                for k in range(FT):
                    pool.wait_ge(m_high, FT * b + k + 1)
                    pool.tensor_tensor(m_lo[slot(k, par)][:], m[k % 2][:], m_hi[slot(k, par)][:].bitcast(F32),
                                       ALU.subtract).then_inc(m_low, 1)
                    if k == 1 and not is_last(b):
                        root(b + 1)
                    if k == 2 and not is_last(b):
                        residual(b + 1, 1 - par)
                    if k == 3 and not (isinstance(b, int) and b == 0):
                        ln_root(b - 1)
                if not (isinstance(b, int) and b + 2 >= B):
                    y2_rest(b + 2)
            over(pool, B, step)
            ln_root(B - 1)

        @block.tensor
        def _(pe):
            pe.wait_ge(par_loaded, 32)
            pe.wait_ge(w_low, 4)

            def out_product(b):
                pe.wait_ge(y2_low, b + 1)
                wait(pe, r_set, b - 1)
                for q in range(QT):
                    toks = slice(q * P, (q + 1) * P)
                    mm = products3(pe, ps_o[:, q, :], [(y2_hi[:, k, toks], y2_lo[:, k, toks]) for k in range(KT)],
                                   [(wo[0][:, k, :], wo[1][:, k, :]) for k in range(KT)])
                mm.then_inc(out_ready, 1)

            def turn(b):
                pe.wait_ge(normed, QT * (b + 1))
                wait(pe, low_set, b)
                for k in range(KT):
                    for q in range(QT):
                        mm = pe.transpose(ps_t[:, k, q * P:(q + 1) * P], yn[:, q, k * P:(k + 1) * P], ident[:])
                mm.then_inc(turned, 1)

            def down(b, par):
                pe.wait_ge(m_low, FT * (b + 1))
                pe.wait_ge(y1_set, b + 2) if not is_last(b) else None
                for q in range(QT):
                    toks = slice(q * P, (q + 1) * P)
                    mm = products3(pe, ps_o[:, q, :],
                                   [(m_hi[slot(k, par)][:, toks], m_lo[slot(k, par)][:, toks]) for k in range(FT)],
                                   [(wd[0][:, k, :], wd[1][:, k, :]) for k in range(FT)])
                mm.then_inc(down_ready, 1)

            out_product(0)
            turn(0)

            def step(b, par):
                pe.wait_ge(low_set, b + 1)
                for k in range(FT):
                    wait(pe, prod_done, FT * b + k - 1)
                    cols = slice(k * FM, (k + 1) * FM)
                    right = [(t_hi[par][:, j, :], t_lo[par][:, j, :]) for j in range(KT)]
                    products3(pe, ps_g[k % 2][0:FM, :], [(wg[0][:, j, cols], wg[1][:, j, cols]) for j in range(KT)], right)
                    products3(pe, ps_u[k % 2][0:FM, :], [(wu[0][:, j, cols], wu[1][:, j, cols]) for j in range(KT)],
                              right).then_inc(fed, 1)
                    if k == 1 and not (isinstance(b, int) and b == 0):
                        down(b - 1, 1 - par)
                    if k == 2 and not is_last(b):
                        out_product(b + 1)
                    if k == 4 and not is_last(b):
                        turn(b + 1)
            over(pe, B, step)
            down(B - 1, 1)

        @block.vector
        def _(dve):
            dve.wait_ge(par_loaded, 32)
            scaled = 0
            for k, (parts, rows, size) in enumerate(((wo, P, KT * D), (wg, P, KT * FF), (wu, P, KT * FF), (wd, FM, FT * D))):
                dve.wait_ge(w_loaded, 16 * (k + 1))
                flat = raw[0:rows, 0:size]
                if k in (1, 2):
                    for j in range(KT):
                        dve.tensor_scalar(raw[:, j * FF:(j + 1) * FF], raw[:, j * FF:(j + 1) * FF], wsc[:, j:j + 1],
                                          None, ALU.mult).then_inc(w_scaled, 1)
                    scaled += KT
                    dve.wait_ge(w_scaled, scaled)
                hi, lo = (t[:].rearrange("p k m -> p (k m)") for t in parts)
                dve.tensor_copy(hi, flat).then_inc(w_high, 1)
                dve.wait_ge(w_high, k + 1)
                dve.tensor_tensor(lo, flat, hi.bitcast(F32), ALU.subtract).then_inc(w_low, 1)

            def prepare(b):
                wait(dve, y2_low, b)
                dve.wait_ge(y_fetched, 16 * (b + 1))
                for k in range(KT):
                    src = turned_y[:, k * C:(k + 1) * C, :].rearrange("p c n -> p n c")
                    dve.transpose(y2[:, k, :].rearrange("p (n c) -> p n c", c=C), src).then_inc(unchunked, 1)
                dve.wait_ge(unchunked, KT * (b + 1))
                dve.wait_ge(x2_loaded, 16 * (b + 1))
                dve.tensor_tensor(y2[:], y2[:], x2[:], ALU.mult).then_inc(gated, 1)

            def add_x(b):
                dve.wait_ge(out_ready, b + 1)
                dve.wait_ge(x_loaded, 16 * (b + 1))
                wait(dve, xy_set, b)
                dve.tensor_tensor(y1[:], ps_o[:], xin[:], ALU.add).then_inc(y1_set, 1)

            def norm(b):
                dve.wait_ge(rstd_set, b + 1)
                for q in range(QT):
                    dve.tensor_scalar(yn[:, q, :], y1[:, q, :], rstd[:, q:q + 1], None, ALU.mult).then_inc(normed, 1)

            def low(b, par):
                dve.wait_ge(high_set, b + 1)
                dve.tensor_tensor(t_lo[par][:], ps_t[:], t_hi[par][:].bitcast(F32), ALU.subtract).then_inc(low_set, 1)

            def add_mlp(b, par):
                dve.wait_ge(down_ready, b + 1)
                dve.wait_ge(xy_set, b + 1)
                wait(dve, x1_stored, 16 * b)
                dve.tensor_tensor(r[:], ps_o[:], xy[par][:], ALU.add).then_inc(r_set, 1)
                dve.wait_ge(r_set, b + 1)
                wait(dve, lnv_set, b)
                for q in range(QT):
                    dve.bn_stats(bn[:, q, :], r[:, q, :]).then_inc(stats, 1)
                for q in range(QT):
                    dve.wait_ge(stats, QT * b + q + 1)
                    settle(dve, dve_settled)
                    dve.bn_aggr(mv[:, q, :], bn[:, q, :]).then_inc(aggr, 1)

            def layernorm(b):
                dve.wait_ge(lnr_set, b + 1)
                for q in range(QT):
                    dve.tensor_scalar(r[:, q, :], r[:, q, :], mv[:, q, 0:1], lnr[:, q:q + 1],
                                      ALU.subtract, ALU.mult).then_inc(x1_set, 1)

            prepare(0)
            add_x(0)
            norm(0)
            low(0, 0)
            prepare(1)

            def step(b, par):
                for k in range(FT):
                    dve.wait_ge(gelu_done, FT * b + k + 1)
                    wait(dve, m_low, FT * b + k - 1)
                    dve.tensor_tensor(m[k % 2][:], gl[k % 2][:], ps_u[k % 2][0:FM, :], ALU.mult).then_inc(prod_done, 1)
                    if k == 1 and not (isinstance(b, int) and b == 0):
                        add_mlp(b - 1, 1 - par)
                    if k == 2 and not is_last(b):
                        add_x(b + 1)
                    if k == 3 and not is_last(b):
                        norm(b + 1)
                    if k == 4 and not is_last(b):
                        low(b + 1, 1 - par)
                if not (isinstance(b, int) and b + 2 >= B):
                    prepare(b + 2)
                if not (isinstance(b, int) and b == 0):
                    layernorm(b - 1)
            over(dve, B, step)
            add_mlp(B - 1, 1)
            layernorm(B - 1)


H, HD, CL, CC = 16, 16, 64, 128
HE = H // KT
ROWS = 6 * HD
V1 = HD + 1
SCALE = float(HD) ** -0.5

UNITS = [(qt, h0, n) for qt, n in enumerate((4, 2, 1, 1)) for h0 in range(0, H, n)]
NU = len(UNITS)
LAST_OF = [max(u for u, (qt, _, _) in enumerate(UNITS) if qt == t) for t in range(QT)]
FIRST_OF = [min(u for u, (qt, _, _) in enumerate(UNITS) if qt == t) for t in range(QT)]
RING = 4
LAG = 2
SLOTS = """t0 t1 q0 k0 q1 k1 y0 y1 c0 c1 p0 p1 kc vc v0 v1 - s0 s1 s2 s3 s4 s5 s6 s7 nc w0 w1 w2 w3 w4 w5 w6 w7 n0
           o0 o1 o2 o3 n1 n2 - - - - n3""".split()
FRONT = [j for j in SLOTS if j[0] not in "yp-"]
TAIL = [j for j in SLOTS if j[0] in "yp"]
NF, NT = len(FRONT), len(TAIL)
S_SLOT = 12
SCORED_IN = [[s for s in range(NU) if S_SLOT + s * (NU - S_SLOT) // NU == u] for u in range(len(SLOTS))]


def view_unit(t, qt, n):
    w = (qt + 1) * P
    return t[:, 0:n * w].rearrange("p (h w) -> p h w", w=w)


def attend(nc, x1_d, ctx_t, w_qkcv, w_ctx, w_proj, b_qkc, b_ck, b_rows, c_ident, c_heads, c_sel,
           parts_d, x2_d):
    with ExitStack() as ctx:
        n = Names(nc, ctx, "at")
        ident, ident16, mask16 = n.sb("ident", [P, P]), n.sb("ident16", [P, P], BF16), n.sb("mask16", [P, P], BF16)
        heads = n.sb("heads", [P, HE])
        sel = n.sb("sel", [H, HE, P], F32R)
        raw = n.sb("raw", [P, KT * D])
        w_hi = [n.sb(f"w_hi{i}", [P, KT, D], F32R) for i in range(5)]
        w_lo = [n.sb(f"w_lo{i}", [P, KT, D], F32R) for i in range(5)]
        wc = n.sb("wc", [P, 2, D])
        bias = n.sb("bias", [P, 3, KT])
        bck = n.sb("bck", [P, KT])
        brow = n.sb("brow", [P, 3, D])
        xin, xb = (n.sb(s, [P, QT, D]) for s in ("xin", "xb"))
        ctx2 = n.sb("ctx2", [P, 2, CL])
        x_hi, x_lo = n.sb("x_hi", [P, KT, T], F32R), n.sb("x_lo", [P, KT, T], F32R)
        parts = [n.sb(f"parts{i}", [P, 3, T], BF16) for i in range(2)]
        rest = [n.sb(f"rest{i}", [P, T]) for i in range(2)]
        qs = [n.sb(f"qs{i}", [ROWS + 1, H, T], BF16) for i in range(2)]
        ks = [n.sb(f"ks{i}", [ROWS + 1, H, T], BF16) for i in range(2)]
        mneg = n.sb("mneg", [P, QT, H])
        mrow = n.sb("mrow", [H, QT, P], BF16)
        val = [n.sb(f"val{i}", [P, QT, H, V1]) for i in range(2)]
        pt = [n.sb(f"pt{i}", [P, 512]) for i in range(RING)]
        cq_hi, cq_lo = n.sb("cq_hi", [P, KT, T], F32R), n.sb("cq_lo", [P, KT, T], F32R)
        kc, kc_lo = n.sb("kc", [P, KT, CL]), n.sb("kc_lo", [P, KT, CL])
        kc_hi = n.sb("kc_hi", [P, KT, CL], F32R)
        km_hi, km_lo = n.sb("km_hi", [P, KT, HE, CL], F32R), n.sb("km_lo", [P, KT, HE, CL], F32R)
        mcneg = n.sb("mcneg", [P, QT, H])
        mcrow = n.sb("mcrow", [H, T], F32R)
        ptc = n.sb("ptc", [P, HE, T])
        valc = n.sb("valc", [P, HE, 2, V1])
        rden, rdenc = n.sb("rden", [P, QT, H]), n.sb("rdenc", [P, QT, H])
        y = [n.sb(f"y{i}", [P, QT, H, HD]) for i in range(2)]
        ys = n.sb("ys", [P, H, HD])
        yt_hi, yt_lo = n.sb("yt_hi", [P, KT, T], F32R), n.sb("yt_lo", [P, KT, T], F32R)
        r = n.sb("r", [P, QT, D])
        mhalf, lnv, lnr = (n.sb(s, [P, QT]) for s in ("mhalf", "lnv", "lnr"))
        bn, mv = n.sb("bn", [P, QT, 6]), n.sb("mv", [P, QT, 2])
        ps_j = n.psum("ps_j", [P, 512])
        ps_o = n.psum("ps_o", [P, 512])
        ps_s = [n.psum(f"ps_s{i}", [P, 512]) for i in range(2)]
        ps_w = [n.psum(f"ps_w{i}", [P, 512]) for i in range(RING)]

        par_loaded, w_loaded, w_high, w_low, const_set, sel_set, ones_set = (
            n.sem(s) for s in ("par_loaded", "w_loaded", "w_high", "w_low", "const_set", "sel_set", "ones_set"))
        x_loaded, ctx_loaded, res_loaded, stacked, x2_stored = (
            n.sem(s) for s in ("x_loaded", "ctx_loaded", "res_loaded", "stacked", "x2_stored"))
        max_placed = [n.sem(f"max_placed{i}") for i in range(QT)]
        parts_out = [n.sem(f"parts_out{i}") for i in range(2)]
        front_ready, front_read, tail_ready, tail_read = (
            n.sem(s) for s in ("front_ready", "front_read", "tail_ready", "tail_read"))
        turn_high, q_high, q_rest, q_mid, q_low = (n.sem(s) for s in ("turn_high", "q_high", "q_rest", "q_mid", "q_low"))
        c_high, kc_parts, kc_low, kc_masked, rdenc_set, vc_half, v_half = (
            n.sem(s) for s in ("c_high", "kc_parts", "kc_low", "kc_masked", "rdenc_set", "vc_half", "v_half"))
        scored, maxed, weighed, exped, cut, summed, rden_set, y_set, y_added = (
            n.sem(s) for s in ("scored", "maxed", "weighed", "exped", "cut", "summed", "rden_set", "y_set", "y_added"))
        y_high, xb_set, stats, aggr, lnv_set, lnr_set, x2_set = (
            n.sem(s) for s in ("y_high", "xb_set", "stats", "aggr", "lnv_set", "lnr_set", "x2_set"))
        pool_settled, dve_settled, sp_settled = (n.sem(s) for s in ("pool_settled", "dve_settled", "sp_settled"))
        block = ctx.enter_context(nc.Block())
        PARS = 7
        CONSTS = 9

        def at(job, b):
            return NT * b + TAIL.index(job) + 1 if job in TAIL else NF * b + FRONT.index(job) + 1

        def slots(b):
            for u, name in enumerate(SLOTS):
                yield u, [j for j in [name] if (j in TAIL and not (isinstance(b, int) and b < 1)) or (j in FRONT and not is_last(b))]

        def back(b):
            return not (isinstance(b, int) and b < 0)

        def over_steps(eng, step):
            step(-1, 1)
            over(eng, B, step)

        @block.sync
        def _(sp):
            for dst, src in ((ident[:], c_ident), (heads[:], c_heads),
                             (r[0:H].rearrange("p q d -> p (q d)"), c_sel), (wc[:], w_ctx), (bias[:], b_qkc), (bck[:], b_ck),
                             (brow[:].rearrange("p k d -> p (k d)"), bass.AP(b_rows.tensor, 0, [[0, P], [1, 3 * D]]))):
                sp.dma_start(dst, src).then_inc(par_loaded, 16)
            for k in range(5):
                wait(sp, w_low, k)
                src = w_qkcv[k] if k < 4 else w_proj
                sp.dma_start(raw[:], src.rearrange("p k m -> p (k m)")).then_inc(w_loaded, 16)

            def load(b):
                wait(sp, front_ready, at("t1", b - 1))
                sp.dma_start(xin[:], x1_d[bass.ds(b, 1)].rearrange("o p q d -> (o p) q d")).then_inc(x_loaded, 16)
                wait(sp, front_ready, at("vc", b - 1))
                for k in range(2):
                    sp.dma_start(ctx2[:, k, :], ctx_t[:, bass.ds(b, 1), :].rearrange("p o s -> p (o s)")).then_inc(ctx_loaded, 16)

            load(0)

            def step(b, par):
                nb, npar = b + 1, 1 - par
                if not is_last(b):
                    for i in range(4):
                        sp.wait_ge(q_low, 4 * nb + i + 1)
                        k, which = i // 2, i % 2
                        sp.dma_start(parts_d[npar, which, k].rearrange("a p t -> p a t"), parts[i % 2][:]).then_inc(parts_out[i % 2], 16)
                    for i in range(2):
                        sp.wait_ge(parts_out[i], 32 * (nb + 1))
                    settle(sp, sp_settled)
                    wait(sp, weighed, NU * (nb - 1))
                    for dst, which, row, part, count in ((qs, 0, 0, 0, 3), (qs, 0, 3, 0, 2), (qs, 0, 5, 0, 1), (ks, 1, 0, 0, 1),
                                                         (ks, 1, 1, 0, 1), (ks, 1, 2, 0, 1), (ks, 1, 3, 1, 1), (ks, 1, 4, 1, 1),
                                                         (ks, 1, 5, 2, 1)):
                        src = parts_d[npar, which, :, part:part + count].rearrange("k a (d e) t -> (a d) k (e t)", e=HE)
                        sp.dma_start(dst[npar][row * HD:(row + count) * HD].rearrange("p (k e) t -> p k (e t)", e=HE),
                                     src).then_inc(stacked, 16)
                    if not (isinstance(b, int) and b + 2 >= B):
                        load(b + 2)
                if not (isinstance(b, int) and b < 1):
                    wait(sp, x2_set, QT * b)
                    sp.dma_start(x2_d[bass.ds(b - 1, 1)].rearrange("o p q d -> (o p) q d"), r[:]).then_inc(x2_stored, 16)
                if not (isinstance(b, int) and b < 0):
                    wait(sp, tail_read, at("p1", b - 1))
                    sp.dma_start(xb[:], x1_d[bass.ds(b, 1)].rearrange("o p q d -> (o p) q d")).then_inc(res_loaded, 16)
                if not is_last(b):
                    for qt in range(QT):
                        sp.wait_ge(front_read, at(f"n{qt}", nb))
                        sp.dma_start(qs[npar][ROWS:ROWS + 1, :, qt * P:(qt + 1) * P], mrow[:, qt, :]).then_inc(max_placed[qt], 16)
            over_steps(sp, step)
            sp.wait_ge(x2_set, QT * B)
            sp.dma_start(x2_d[B - 1], r[:]).then_inc(x2_stored, 16)
            sp.wait_ge(x2_stored, 16 * B)

        @block.tensor
        def _(pe):
            pe.wait_ge(par_loaded, 16 * PARS)
            pe.wait_ge(w_low, 5)
            pe.wait_ge(const_set, CONSTS)
            pe.wait_ge(sel_set, 1)
            pe.wait_ge(ones_set, 2)

            def pairs(hi, lo, index):
                return [(hi[:, k, index], lo[:, k, index]) for k in range(KT)]

            def job(name, b, npar):
                kind, i = name[0], int(name[1]) if name[1].isdigit() else 0
                everything = slice(0, T)
                if kind == "t":
                    pe.wait_ge(x_loaded, 16 * (b + 1))
                    for q in range(QT):
                        mm = pe.transpose(ps_j[:, q * P:(q + 1) * P], xin[:, q, i * P:(i + 1) * P], ident[:])
                elif name in ("kc", "vc"):
                    pe.wait_ge(ctx_loaded, 32 * (b + 1))
                    if name == "kc":
                        for k in range(KT):
                            mm = pe.matmul(ps_j[:, k * CL:(k + 1) * CL], wc[:, 0, k * P:(k + 1) * P], ctx2[:, 0, :],
                                           start=True, stop=True)
                    else:
                        mm = pe.matmul(ps_j[:, 0:D], ctx2[:].rearrange("p a s -> p (a s)"), wc[:, 1, :], start=True, stop=True)
                elif kind in "qkc":
                    w = "qkc".index(kind)
                    pe.wait_ge(front_read, at("t1", b))
                    mm = products3(pe, ps_j[:], pairs(w_hi[w], w_lo[w], slice(i * P, (i + 1) * P)), pairs(x_hi, x_lo, everything))
                elif kind == "v":
                    for q in (2 * i, 2 * i + 1):
                        mm = products3(pe, ps_j[:, (q % 2) * D:(q % 2 + 1) * D], pairs(x_hi, x_lo, slice(q * P, (q + 1) * P)),
                                       pairs(w_hi[3], w_lo[3], slice(0, D)))
                elif kind == "s":
                    qt, k = i // 2, i % 2
                    toks = slice(qt * P, (qt + 1) * P)
                    pe.wait_ge(front_read, at("c1", b))
                    pe.wait_ge(kc_masked, 4 * (b + 1))
                    mm = products3(pe, ps_j[:], [(cq_hi[:, k, toks], cq_lo[:, k, toks])],
                                   [(km_hi[:, k].rearrange("p e s -> p (e s)"), km_lo[:, k].rearrange("p e s -> p (e s)"))])
                elif name == "nc":
                    pe.wait_ge(front_read, at("s7", b))
                    for q in range(QT):
                        mm = pe.transpose(ps_j[0:H, q * P:(q + 1) * P], mcneg[:, q, :], ident[:])
                elif kind == "n":
                    pe.wait_ge(maxed, 2 * NU * b + 2 * (LAST_OF[i] + 1))
                    mm = pe.transpose(ps_j[0:H, 0:P], mneg[:, i, :], ident[:])
                elif kind == "w":
                    k, e = i // 4, 2 * (i % 4)
                    products3(pe, ps_j[:], [(km_hi[:, k, e:e + 2, :].rearrange("p e s -> p (e s)"),
                                             km_lo[:, k, e:e + 2, :].rearrange("p e s -> p (e s)"))],
                              [(cq_hi[:, k, :], cq_lo[:, k, :])], last=False)
                    pe.wait_ge(front_read, at("nc", b))
                    mm = pe.matmul(ps_j[:], sel[:, i, :], mcrow[:], start=False, stop=True)
                elif kind == "o":
                    pe.wait_ge(front_read, at("w7", b))
                    for k in range(HE):
                        mm = pe.matmul(ps_j[:, k * 2 * V1:(k + 1) * 2 * V1], ptc[:, k, i * P:(i + 1) * P],
                                       valc[:, k].rearrange("p a v -> p (a v)"), start=True, stop=True)
                elif kind == "y":
                    pe.wait_ge(y_added, QT * (b + 1))
                    for q in range(QT):
                        mm = pe.transpose(ps_j[:, q * P:(q + 1) * P],
                                          y[npar][:, q].rearrange("p h d -> p (h d)")[:, i * P:(i + 1) * P], ident[:])
                elif kind == "p":
                    pe.wait_ge(tail_read, at("y1", b))
                    for q in (2 * i, 2 * i + 1):
                        mm = products3(pe, ps_j[:, (q % 2) * D:(q % 2 + 1) * D], pairs(yt_hi, yt_lo, slice(q * P, (q + 1) * P)),
                                       pairs(w_hi[4], w_lo[4], slice(0, D)))
                mm.then_inc(tail_ready if name in TAIL else front_ready, 1)

            def scores(b, par, u):
                qt, h0, count = UNITS[u]
                out = view_unit(ps_s[u % 2], qt, count)
                if u == 0:
                    pe.wait_ge(stacked, 9 * 16 * (b + 1))
                wait(pe, maxed, 2 * NU * b + 2 * (u - 1))
                toks = slice(qt * P, (qt + 1) * P)
                for i in range(count):
                    h = h0 + i
                    pe.matmul(out[:, i, :], qs[par][0:ROWS, h, toks], ks[par][0:ROWS, h, 0:(qt + 1) * P], start=True, stop=False)
                    mm = pe.matmul(out[:, i, toks], ident16[:], mask16[:], start=False, stop=True)
                mm.then_inc(scored, 1)

            def weights(b, par, u):
                qt, h0, count = UNITS[u]
                out = view_unit(ps_w[u % RING], qt, count)
                if u == FIRST_OF[qt]:
                    pe.wait_ge(max_placed[qt], 16 * (b + 1))
                wait(pe, exped, NU * b + u - RING + 1)
                toks = slice(qt * P, (qt + 1) * P)
                for i in range(count):
                    h = h0 + i
                    for kt in range(qt + 1):
                        mm = pe.matmul(out[:, i, kt * P:(kt + 1) * P], ks[par][:, h, kt * P:(kt + 1) * P], qs[par][:, h, toks],
                                       start=True, stop=True)
                mm.then_inc(weighed, 1)

            def outputs(b, par, u):
                qt, h0, count = UNITS[u]
                left = view_unit(pt[u % RING], qt, count)
                pe.wait_ge(cut, NU * b + u + 1)
                if u == FIRST_OF[qt]:
                    wait(pe, y_set, QT * b + qt)
                    pe.wait_ge(front_read, at("v1", b))
                for i in range(count):
                    h = h0 + i
                    for kt in range(qt + 1):
                        mm = pe.matmul(ps_o[:, h * V1:(h + 1) * V1], left[:, i, kt * P:(kt + 1) * P], val[par][:, kt, h, :],
                                       start=kt == 0, stop=kt == qt)
                mm.then_inc(summed, 1)

            def step(b, par):
                before = (front_read, NF * (b + 1))
                for u, jobs in slots(b):
                    if back(b) and u < NU:
                        weights(b, par, u)
                    for name in jobs:
                        wait(pe, *before)
                        jb = b - 1 if name in TAIL else b + 1
                        job(name, jb, 1 - par)
                        before = (tail_read if name in TAIL else front_read, at(name, jb))
                    if back(b) and u >= LAG:
                        outputs(b, par, u - LAG)
                    if not is_last(b):
                        for s in SCORED_IN[u]:
                            scores(b + 1, 1 - par, s)
            over_steps(pe, step)
            before = (tail_read, NT * (B - 1))
            for name in TAIL:
                pe.wait_ge(*before)
                job(name, B - 1, 1)
                before = (tail_read, at(name, B - 1))

        @block.scalar
        def _(act):
            act.wait_ge(par_loaded, 16 * PARS)
            act.activation(sel[:].rearrange("h e p -> h (e p)"), r[0:H].rearrange("p q d -> p (q d)"), ACT.Copy).then_inc(sel_set, 1)

            def job(name, b):
                kind, i = name[0], int(name[1]) if name[1].isdigit() else 0
                if kind not in "vspo" or name == "nc":
                    act.wait_ge(tail_ready if name in TAIL else front_ready, at(name, b))
                if kind == "t":
                    if i == 0:
                        wait(act, front_ready, at("v1", b - 1))
                    act.activation(x_hi[:, i, :], ps_j[:], ACT.Copy).then_inc(turn_high, 1)
                elif name == "kc":
                    wait(act, kc_masked, 4 * b)
                    for k in range(KT):
                        act.activation(kc[:, k, :], ps_j[:, k * CL:(k + 1) * CL], ACT.Identity,
                                       bias=bck[:, k:k + 1]).then_inc(front_read if k == KT - 1 else kc_parts, 1)
                    act.wait_ge(front_read, at("kc", b))
                    act.wait_ge(kc_parts, 2 * b + 1)
                    act.activation(kc_hi[:], kc[:], ACT.Copy).then_inc(kc_parts, 1)
                elif kind in "qk":
                    number = 4 * b + ("q0", "k0", "q1", "k1").index(name)
                    w = "qk".index(kind)
                    wait(act, parts_out[w], 16 * (2 * b + i))
                    act.activation(parts[w][:, 0, :], ps_j[:], ACT.Identity, bias=bias[:, w, i:i + 1]).then_inc(q_high, 1)
                elif kind == "c":
                    if i == 0:
                        wait(act, front_ready, at("w7", b - 1))
                    act.activation(cq_hi[:, i, :], ps_j[:], ACT.Identity, bias=bias[:, 2, i:i + 1]).then_inc(c_high, 1)
                elif name == "nc":
                    wait(act, front_ready, at("w7", b - 1))
                    act.activation(mcrow[:], ps_j[0:H, :], ACT.Copy).then_inc(front_read, 1)
                elif kind == "n":
                    wait(act, max_placed[i], 16 * b)
                    act.activation(mrow[:, i, :], ps_j[0:H, 0:P], ACT.Copy).then_inc(front_read, 1)
                elif kind == "w":
                    if i == 0:
                        wait(act, front_ready, at("o3", b - 1))
                    act.activation(ptc[:, i, :], ps_j[:], ACT.Exp, scale=SCALE).then_inc(front_read, 1)
                elif kind == "y":
                    if i == 0:
                        wait(act, tail_ready, at("p1", b - 1))
                    act.activation(yt_hi[:, i, :], ps_j[:], ACT.Copy).then_inc(y_high, 1)

            def middle(name, b):
                w, i = "qk".index(name[0]), int(name[1])
                act.wait_ge(front_read, at(name, b))
                act.activation(parts[w][:, 1, :], rest[w][:], ACT.Copy).then_inc(q_mid, 1)

            def step(b, par):
                for u, jobs in slots(b):
                    if back(b) and u < NU:
                        qt, h0, count = UNITS[u]
                        act.wait_ge(weighed, NU * b + u + 1)
                        wait(act, summed, NU * b + u - RING + 1)
                        act.activation(view_unit(pt[u % RING], qt, count), view_unit(ps_w[u % RING], qt, count), ACT.Exp,
                                       scale=SCALE).then_inc(exped, 1)
                    for name in jobs:
                        job(name, b - 1 if name in TAIL else b + 1)
                    for name in jobs:
                        if name[0] in "qk" and name != "kc":
                            middle(name, b + 1)
            over_steps(act, step)
            for name in TAIL:
                job(name, B - 1)

        @block.gpsimd
        def _(pool):
            pool.memset(mhalf[:], -0.5).then_inc(const_set, 1)
            for i in range(2):
                pool.memset(val[i][:], 1.0).then_inc(const_set, 1)
            pool.memset(valc[:], 0.0).then_inc(const_set, 1)
            pool.wait_ge(const_set, 4)
            for k in range(2):
                pool.memset(valc[k * CL:(k + 1) * CL, :, k, HD:V1], 1.0).then_inc(const_set, 1)
            pool.wait_ge(const_set, 6)
            pool.memset(mask16[:], 0.0).then_inc(const_set, 1)
            pool.wait_ge(const_set, 7)
            pool.affine_select(out=mask16[:], in_=mask16[:], compare_op=ALU.is_ge, fill=-1e30, base=0,
                               pattern=[[-1, P]], channel_multiplier=1).then_inc(const_set, 1)
            pool.wait_ge(par_loaded, 16 * PARS)
            pool.wait_ge(const_set, 8)
            pool.tensor_copy(ident16[:], ident[:]).then_inc(const_set, 1)
            pool.wait_ge(const_set, CONSTS)

            def low_part(name, b):
                w = "qk".index(name[0])
                pool.wait_ge(q_mid, 4 * b + ("q0", "k0", "q1", "k1").index(name) + 1)
                pool.tensor_tensor(parts[w][:, 2, :], rest[w][:], parts[w][:, 1, :], ALU.subtract).then_inc(q_low, 1)

            def context_keys(b, piece):
                if piece == 0:
                    pool.wait_ge(kc_parts, 2 * b + 2)
                    wait(pool, kc_masked, 4 * b)
                    pool.tensor_tensor(kc_lo[:], kc[:], kc_hi[:].bitcast(F32), ALU.subtract).then_inc(kc_low, 1)
                    wait(pool, front_ready, at("w7", b - 1))
                else:
                    k = (piece - 1) % KT
                    if piece == 1:
                        pool.wait_ge(kc_low, b + 1)
                    src, dst = ((kc_hi[:].bitcast(F32), km_hi), (kc_lo[:], km_lo))[(piece - 1) // KT]
                    pool.tensor_tensor(dst[:, k], src[:, k, :].unsqueeze(1).to_broadcast([P, HE, CL]),
                                       heads[:].unsqueeze(2).to_broadcast([P, HE, CL]), ALU.mult).then_inc(kc_masked, 1)

            def ln_root(b):
                pool.wait_ge(aggr, QT * (b + 1))
                settle(pool, pool_settled)
                pool.tensor_scalar(lnv[:], mv[:, :, 1], 1.0, LN_EPS, ALU.mult, ALU.add).then_inc(lnv_set, 1)
                pool.wait_ge(lnv_set, b + 1)
                wait(pool, x2_set, QT * b)
                pool.tensor_tensor(lnr[:], lnv[:], mhalf[:], ALU.pow).then_inc(lnr_set, 1)

            def residual(b):
                pool.wait_ge(res_loaded, 16 * (b + 1))
                pool.tensor_tensor(xb[:], xb[:], brow[:, 2:3, :].to_broadcast([P, QT, D]), ALU.add).then_inc(xb_set, 1)

            def step(b, par):
                for u, jobs in slots(b):
                    if back(b) and u < NU:
                        qt, h0, count = UNITS[u]
                        pool.wait_ge(exped, NU * b + u + 1)
                        settle(pool, pool_settled)
                        diag = view_unit(pt[u % RING], qt, count)[:, :, qt * P:(qt + 1) * P]
                        pool.affine_select(out=diag, in_=diag, compare_op=ALU.is_ge, fill=0.0, base=0,
                                           pattern=[[0, count], [1, P]], channel_multiplier=-1).then_inc(cut, 1)
                    for name in jobs:
                        if name[0] in "qk" and name != "kc":
                            low_part(name, b + 1)
                    if 0 <= u - SLOTS.index("kc") <= 2 * KT and not is_last(b):
                        context_keys(b + 1, u - SLOTS.index("kc"))
                    if u == SLOTS.index("p1") + 1 and not (isinstance(b, int) and b < 1):
                        ln_root(b - 1)
                    if u == NU - 3 and back(b):
                        residual(b)
            over_steps(pool, step)
            ln_root(B - 1)

        @block.vector
        def _(dve):
            for i in range(2):
                dve.memset(ks[i][ROWS:ROWS + 1], 1.0).then_inc(ones_set, 1)
            for k in range(5):
                dve.wait_ge(w_loaded, 16 * (k + 1))
                hi, lo = (t[k][:].rearrange("p k m -> p (k m)") for t in (w_hi, w_lo))
                dve.tensor_copy(hi, raw[:]).then_inc(w_high, 1)
                dve.wait_ge(w_high, k + 1)
                dve.tensor_tensor(lo, raw[:], hi.bitcast(F32), ALU.subtract).then_inc(w_low, 1)
            dve.wait_ge(par_loaded, 16 * PARS)
            dve.wait_ge(const_set, CONSTS)
            dve.wait_ge(sel_set, 1)

            def job(name, b, npar):
                kind, i = name[0], int(name[1]) if name[1].isdigit() else 0
                if kind == "t":
                    dve.wait_ge(turn_high, 2 * b + i + 1)
                    if i == 0:
                        wait(dve, front_ready, at("v1", b - 1))
                    dve.tensor_tensor(x_lo[:, i, :], ps_j[:], x_hi[:, i, :].bitcast(F32), ALU.subtract).then_inc(front_read, 1)
                elif name == "vc":
                    dve.wait_ge(front_ready, at("vc", b))
                    wait(dve, front_ready, at("o3", b - 1))
                    for k in range(2):
                        rows = slice(k * CL, (k + 1) * CL)
                        src = ps_j[rows, 0:D].rearrange("p (g a d) -> p g a d", a=2, d=HD)[:, :, k, :]
                        add = brow[rows, 1, :].rearrange("p (g a d) -> p g a d", a=2, d=HD)[:, :, k, :]
                        dve.tensor_tensor(valc[rows, :, k, 0:HD], src, add, ALU.add).then_inc(front_read if k else vc_half, 1)
                elif kind in "qk" and name != "kc":
                    number = 4 * b + ("q0", "k0", "q1", "k1").index(name)
                    w = "qk".index(kind)
                    dve.wait_ge(q_high, number + 1)
                    wait(dve, q_low, number - 1)
                    dve.scalar_tensor_tensor(rest[w][:], ps_j[:], bias[:, w, i:i + 1], parts[w][:, 0, :],
                                             ALU.add, ALU.subtract).then_inc(front_read, 1)
                elif kind == "c":
                    dve.wait_ge(c_high, 2 * b + i + 1)
                    dve.scalar_tensor_tensor(cq_lo[:, i, :], ps_j[:], bias[:, 2, i:i + 1], cq_hi[:, i, :].bitcast(F32),
                                             ALU.add, ALU.subtract).then_inc(front_read, 1)
                elif kind == "v":
                    dve.wait_ge(front_ready, at(name, b))
                    wait(dve, summed, NU * (b - 1))
                    src = ps_j[:].rearrange("p (q h d) -> p q h d", q=2, d=HD)
                    add = brow[:, 0, :].rearrange("p (h d) -> p h d", d=HD)
                    for q in range(2):
                        dve.tensor_tensor(val[npar][:, 2 * i + q, :, 0:HD], src[:, q], add, ALU.add)\
                           .then_inc(front_read if q else v_half, 1)
                elif kind == "s":
                    qt, k = i // 2, i % 2
                    dve.wait_ge(front_ready, at(name, b))
                    wait(dve, front_ready, at("nc", b - 1))
                    dve.tensor_reduce(mcneg[:, qt, k * HE:(k + 1) * HE], ps_j[:].rearrange("p (e s) -> p e s", s=CL), AX_X,
                                      ALU.max, negate=True).then_inc(front_read, 1)
                elif kind == "o":
                    dve.wait_ge(front_ready, at(name, b))
                    src = ps_j[:, 0:H * V1].rearrange("p (h v) -> p h v", v=V1)
                    if i == 0:
                        wait(dve, tail_ready, at("y1", b - 2))
                    dve.reciprocal(rdenc[:, i, :], src[:, :, HD]).then_inc(rdenc_set, 1)
                    dve.wait_ge(rdenc_set, QT * b + i + 1)
                    dve.tensor_tensor(y[npar][:, i], src[:, :, 0:HD], rdenc[:, i, :].unsqueeze(2).to_broadcast([P, H, HD]),
                                      ALU.mult).then_inc(front_read, 1)
                elif kind == "y":
                    dve.wait_ge(y_high, 2 * b + i + 1)
                    dve.tensor_tensor(yt_lo[:, i, :], ps_j[:], yt_hi[:, i, :].bitcast(F32), ALU.subtract).then_inc(tail_read, 1)
                elif kind == "p":
                    dve.wait_ge(tail_ready, at(name, b))
                    dve.wait_ge(xb_set, b + 1)
                    wait(dve, x2_stored, 16 * b)
                    dve.tensor_tensor(r[:, 2 * i:2 * i + 2, :].rearrange("p q d -> p (q d)"), ps_j[:],
                                      xb[:, 2 * i:2 * i + 2, :].rearrange("p q d -> p (q d)"), ALU.add).then_inc(tail_read, 1)
                    if i == 1:
                        dve.wait_ge(tail_read, at("p1", b))
                        wait(dve, lnv_set, b)
                        for q in range(QT):
                            dve.bn_stats(bn[:, q, :], r[:, q, :]).then_inc(stats, 1)
                        for q in range(QT):
                            dve.wait_ge(stats, QT * b + q + 1)
                            settle(dve, dve_settled)
                            dve.bn_aggr(mv[:, q, :], bn[:, q, :]).then_inc(aggr, 1)

            def layernorm(b):
                dve.wait_ge(lnr_set, b + 1)
                for q in range(QT):
                    dve.tensor_scalar(r[:, q, :], r[:, q, :], mv[:, q, 0:1], lnr[:, q:q + 1],
                                      ALU.subtract, ALU.mult).then_inc(x2_set, 1)

            def divide(b, par, qt):
                dve.wait_ge(summed, NU * b + LAST_OF[qt] + 1)
                src = ps_o[:, 0:H * V1].rearrange("p (h v) -> p h v", v=V1)
                wait(dve, y_added, QT * b + qt)
                dve.reciprocal(rden[:, qt, :], src[:, :, HD]).then_inc(rden_set, 1)
                dve.wait_ge(rden_set, QT * b + qt + 1)
                dve.tensor_tensor(ys[:], src[:, :, 0:HD], rden[:, qt, :].unsqueeze(2).to_broadcast([P, H, HD]),
                                  ALU.mult).then_inc(y_set, 1)
                dve.wait_ge(y_set, QT * b + qt + 1)
                dve.tensor_tensor(y[par][:, qt], y[par][:, qt], ys[:], ALU.add).then_inc(y_added, 1)

            def step(b, par):
                for u, jobs in slots(b):
                    for place, name in enumerate(jobs):
                        if name[0] == "n":
                            continue
                        job(name, b - 1 if name in TAIL else b + 1, 1 - par)
                    if back(b) and (u - LAG) in LAST_OF:
                        divide(b, par, LAST_OF.index(u - LAG))
                    if u == SLOTS.index("p1") + 3 and not (isinstance(b, int) and b < 1):
                        layernorm(b - 1)
                    if not is_last(b):
                        for s in SCORED_IN[u]:
                            qt, h0, count = UNITS[s]
                            dve.wait_ge(scored, NU * (b + 1) + s + 1)
                            wait(dve, front_ready, at(f"n{qt}", b))
                            dve.tensor_reduce(mneg[:, qt, h0:h0 + count], view_unit(ps_s[s % 2], qt, count), AX_X, ALU.max,
                                              negate=True).then_inc(maxed, 2)
            over_steps(dve, step)
            for name in TAIL:
                job(name, B - 1, 1)
            layernorm(B - 1)


RANK, HID = 64, 1024
HT = HID // P


def ffn(nc, x2_d, w_u1, w_v1, b1, w_u2, w_v2, b2, c_ident, out):
    with ExitStack() as ctx:
        n = Names(nc, ctx, "ff")
        ident = n.sb("ident", [P, P])
        raw_u1 = n.sb("raw_u1", [P, KT, 2, RANK])
        raw_v1 = n.sb("raw_v1", [P, HID])
        raw_u2 = n.sb("raw_u2", [P, HT, RANK])
        raw_v2 = n.sb("raw_v2", [P, D])
        u1 = [n.sb(f"u1{i}", [P, KT, 2 * RANK], F32R) for i in range(2)]
        v1 = [n.sb(f"v1{i}", [P, HID], F32R) for i in range(2)]
        u2 = [n.sb(f"u2{i}", [P, HT, 2, RANK], F32R) for i in range(2)]
        v2 = [n.sb(f"v2{i}", [P, D], F32R) for i in range(2)]
        bias1 = n.sb("bias1", [P, HT])
        bias2 = n.sb("bias2", [P, D])
        xin = [n.sb(f"xin{i}", [P, QT, D]) for i in range(2)]
        xb = [n.sb(f"xb{i}", [P, QT, D]) for i in range(2)]
        x_hi = [n.sb(f"x_hi{i}", [P, KT, T], F32R) for i in range(2)]
        x_lo = [n.sb(f"x_lo{i}", [P, KT, T], F32R) for i in range(2)]
        pp = [n.sb(f"pp{i}", [P, T], F32R) for i in range(2)]
        hid = [n.sb(f"hid{i}", [P, T]) for i in range(4)]
        h_hi = [n.sb(f"h_hi{i}", [P, T], F32R) for i in range(4)]
        h_lo = [n.sb(f"h_lo{i}", [P, T], F32R) for i in range(4)]
        q_hi = [n.sb(f"q_hi{i}", [P, T], F32R) for i in range(2)]
        q_lo = [n.sb(f"q_lo{i}", [P, T], F32R) for i in range(2)]
        r = [n.sb(f"r{i}", [P, QT, D]) for i in range(2)]
        mhalf = n.sb("mhalf", [P, QT])
        lnv = [n.sb(f"lnv{i}", [P, QT]) for i in range(2)]
        lnr = [n.sb(f"lnr{i}", [P, QT]) for i in range(2)]
        bn = n.sb("bn", [P, QT, 6])
        mv = [n.sb(f"mv{i}", [P, QT, 2]) for i in range(2)]
        ps_t = n.psum("ps_t", [P, T])
        ps_p = n.psum("ps_p", [P, T])
        ps_h = [n.psum(f"ps_h{i}", [P, T]) for i in range(2)]
        ps_q = n.psum("ps_q", [P, T])
        ps_o = n.psum("ps_o", [P, QT, D])
        par_loaded, w_high, w_split, const_set = (n.sem(s) for s in ("par_loaded", "w_high", "w_split", "const_set"))
        x_loaded = [n.sem(f"x_loaded{i}") for i in range(2)]
        stored = [n.sem(f"stored{i}") for i in range(2)]
        turned, high_set, low_set, xb_set, p_ready, p_high, p_split = (
            n.sem(s) for s in ("turned", "high_set", "low_set", "xb_set", "p_ready", "p_high", "p_split"))
        h_ready, gelu_done, hid_high, q_ready, q_high, q_low = (
            n.sem(s) for s in ("h_ready", "gelu_done", "hid_high", "q_ready", "q_high", "q_low"))
        hid_low = [n.sem(f"hid_low{i}") for i in range(2)]
        o_ready, r_set, stats, aggr, lnv_set, lnr_set, out_set = (
            n.sem(s) for s in ("o_ready", "r_set", "stats", "aggr", "lnv_set", "lnr_set", "out_set"))
        pool_settled, dve_settled = n.sem("pool_settled"), n.sem("dve_settled")
        block = ctx.enter_context(nc.Block())
        RING = 4

        @block.sync
        def _(sp):
            for dst, src in ((ident[:], c_ident), (raw_u1[:, :, 0, :], w_u1), (raw_u1[:, :, 1, :], w_u1),
                             (raw_v1[0:RANK, :], w_v1), (raw_v1[RANK:P, :], w_v1), (raw_u2[:], w_u2),
                             (raw_v2[0:RANK, :], w_v2), (raw_v2[RANK:P, :], w_v2), (bias1[:], b1),
                             (bias2[:], bass.AP(b2.tensor, 0, [[0, P], [1, D]]))):
                sp.dma_start(dst, src).then_inc(par_loaded, 16)

            def load(b, par):
                wait(sp, turned, KT * (b - 1))
                wait(sp, xb_set, b - 1)
                sp.dma_start(xin[par][:], x2_d[bass.ds(b, 1)].rearrange("o p q d -> (o p) q d")).then_inc(x_loaded[par], 16)

            def store(b, par):
                sp.wait_ge(out_set, QT * (b + 1))
                sp.dma_start(out[bass.ds(b, 1)].rearrange("o (q p) d -> p (o q) d", p=P), r[par][:]).then_inc(stored[par], 16)

            load(0, 0)
            load(1, 1)

            def step(b, par):
                if not (isinstance(b, int) and b + 2 >= B):
                    load(b + 2, par)
                if not (isinstance(b, int) and b == 0):
                    store(b - 1, 1 - par)
            over(sp, B, step)
            store(B - 1, 1)
            for i in range(2):
                sp.wait_ge(stored[i], 16 * (B // 2))

        @block.tensor
        def _(pe):
            pe.wait_ge(par_loaded, 160)
            pe.wait_ge(w_split, 7)

            def turn(b, par, k):
                pe.wait_ge(x_loaded[par], loads(b, par))
                wait(pe, low_set, KT * b + k)
                for q in range(QT):
                    mm = pe.transpose(ps_t[:, q * P:(q + 1) * P], xin[par][:, q, k * P:(k + 1) * P], ident[:])
                mm.then_inc(turned, 1)

            def first(b, par):
                pe.wait_ge(low_set, KT * (b + 1))
                wait(pe, p_split, b)
                products3(pe, ps_p[:], [(u1[0][:, k, :], u1[1][:, k, :]) for k in range(KT)],
                          [(x_hi[par][:, k, :], x_lo[par][:, k, :]) for k in range(KT)]).then_inc(p_ready, 1)

            def hidden(b, par, k):
                if k == 0:
                    pe.wait_ge(p_split, b + 1)
                cols = slice(k * P, (k + 1) * P)
                wait(pe, gelu_done, HT * b + k - 1)
                pe.matmul(ps_h[k % 2][:], v1[0][:, cols], pp[par][:], start=True, stop=False)
                pe.matmul(ps_h[k % 2][:], v1[1][:, cols], pp[par][:], start=False, stop=True).then_inc(h_ready, 1)

            def second(b, k):
                pe.wait_ge(hid_low[k % 2], HT // 2 * b + k // 2 + 1)
                if k == 0:
                    wait(pe, q_low, b)
                left = [u2[i][:, k].rearrange("p a r -> p (a r)") for i in range(2)]
                pe.matmul(ps_q[:], left[0], h_hi[k % RING][:], start=k == 0, stop=False)
                pe.matmul(ps_q[:], left[1], h_lo[k % RING][:], start=False, stop=k == HT - 1).then_inc(q_ready, 1)

            def last_product(b, par):
                pe.wait_ge(q_low, b + 1)
                wait(pe, r_set, b)
                for q in range(QT):
                    toks = slice(q * P, (q + 1) * P)
                    mm = products3(pe, ps_o[:, q, :], [(q_hi[par][:, toks], q_lo[par][:, toks])], [(v2[0][:], v2[1][:])])
                mm.then_inc(o_ready, 1)

            for k in range(KT):
                turn(0, 0, k)
            first(0, 0)

            def step(b, par):
                for k in range(HT):
                    hidden(b, par, k)
                    if k == 1 and not (isinstance(b, int) and b == 0):
                        second(b - 1, HT - 2)
                        second(b - 1, HT - 1)
                    if k == 2 and not (isinstance(b, int) and b == 0):
                        last_product(b - 1, 1 - par)
                    if k >= 2:
                        second(b, k - 2)
                    if not is_last(b):
                        if k in (3, 4):
                            turn(b + 1, 1 - par, k - 3)
                        if k == 6:
                            first(b + 1, 1 - par)
            over(pe, B, step)
            second(B - 1, HT - 2)
            second(B - 1, HT - 1)
            last_product(B - 1, 1)

        @block.scalar
        def _(act):
            act.wait_ge(par_loaded, 160)

            def high(b, par, k):
                act.wait_ge(turned, KT * b + k + 1)
                wait(act, p_ready, b - 1)
                act.activation(x_hi[par][:, k, :], ps_t[:], ACT.Copy).then_inc(high_set, 1)

            def first_high(b, par):
                act.wait_ge(p_ready, b + 1)
                wait(act, h_ready, HT * (b - 1))
                act.activation(pp[par][:], ps_p[:], ACT.Copy).then_inc(p_high, 1)

            def second_high(b, par):
                act.wait_ge(q_ready, HT * (b + 1))
                wait(act, o_ready, b - 1)
                act.activation(q_hi[par][:], ps_q[:], ACT.Copy).then_inc(q_high, 1)

            high(0, 0, 0)
            high(0, 0, 1)
            first_high(0, 0)

            def step(b, par):
                for k in range(HT):
                    act.wait_ge(h_ready, HT * b + k + 1)
                    wait(act, hid_low[k % 2], HT // 2 * b + (k - RING) // 2 + 1)
                    act.activation(hid[k % RING][:], ps_h[k % 2][:], ACT.Gelu_apprx_tanh, bias=bias1[:, k:k + 1]).then_inc(gelu_done, 1)
                    if k == 2 and not (isinstance(b, int) and b == 0):
                        second_high(b - 1, 1 - par)
                    if not is_last(b):
                        if k in (3, 4):
                            high(b + 1, 1 - par, k - 3)
                        if k == 6:
                            first_high(b + 1, 1 - par)
            over(act, B, step)
            second_high(B - 1, 1)

        @block.gpsimd
        def _(pool):
            pool.memset(mhalf[:], -0.5).then_inc(const_set, 1)
            pool.wait_ge(const_set, 1)
            pool.wait_ge(par_loaded, 160)

            def residual(b, par):
                pool.wait_ge(x_loaded[par], loads(b, par))
                wait(pool, r_set, b - 1)
                pool.tensor_tensor(xb[par][:], xin[par][:], bias2[:].unsqueeze(1).to_broadcast([P, QT, D]), ALU.add).then_inc(xb_set, 1)

            def ln_root(b, par):
                pool.wait_ge(aggr, QT * (b + 1))
                settle(pool, pool_settled)
                pool.tensor_scalar(lnv[par][:], mv[par][:, :, 1], 1.0, LN_EPS, ALU.mult, ALU.add).then_inc(lnv_set, 1)
                pool.wait_ge(lnv_set, b + 1)
                wait(pool, out_set, QT * (b - 1))
                pool.tensor_tensor(lnr[par][:], lnv[par][:], mhalf[:], ALU.pow).then_inc(lnr_set, 1)

            residual(0, 0)

            def step(b, par):
                for k in range(1, HT, 2):
                    pool.wait_ge(hid_high, HT * b + k + 1)
                    pool.tensor_tensor(h_lo[k % RING][:], hid[k % RING][:], h_hi[k % RING][:].bitcast(F32),
                                       ALU.subtract).then_inc(hid_low[1], 1)
                    if k == 3 and not (isinstance(b, int) and b == 0):
                        ln_root(b - 1, 1 - par)
                    if k == 5 and not is_last(b):
                        residual(b + 1, 1 - par)
            over(pool, B, step)
            ln_root(B - 1, 1)

        @block.vector
        def _(dve):
            dve.memset(v1[1][RANK:P, :].bitcast(F32), 0.0).then_inc(w_split, 1)
            dve.memset(u2[1][:, :, 1, :].bitcast(F32), 0.0).then_inc(w_split, 1)
            dve.wait_ge(par_loaded, 160)
            flat_u1 = raw_u1[:].rearrange("p k a r -> p (k a r)")
            dve.tensor_copy(u1[0][:].rearrange("p k m -> p (k m)"), flat_u1).then_inc(w_high, 1)
            dve.tensor_copy(v1[0][:], raw_v1[:]).then_inc(w_high, 1)
            dve.tensor_copy(u2[0][:, :, 0, :], raw_u2[:]).then_inc(w_high, 1)
            dve.tensor_copy(v2[0][:], raw_v2[:]).then_inc(w_high, 1)
            dve.wait_ge(w_high, 4)
            dve.tensor_tensor(u1[1][:].rearrange("p k m -> p (k m)"), flat_u1,
                              u1[0][:].rearrange("p k m -> p (k m)").bitcast(F32), ALU.subtract).then_inc(w_split, 1)
            dve.tensor_tensor(v1[1][0:RANK, :], raw_v1[0:RANK, :], v1[0][0:RANK, :].bitcast(F32), ALU.subtract).then_inc(w_split, 1)
            dve.tensor_tensor(u2[0][:, :, 1, :], raw_u2[:], u2[0][:, :, 0, :].bitcast(F32), ALU.subtract).then_inc(w_split, 1)
            dve.tensor_copy(u2[1][:, :, 0, :], raw_u2[:]).then_inc(w_split, 1)
            dve.tensor_tensor(v2[1][:], raw_v2[:], v2[0][:].bitcast(F32), ALU.subtract).then_inc(w_split, 1)

            def low(b, par, k):
                dve.wait_ge(high_set, KT * b + k + 1)
                dve.tensor_tensor(x_lo[par][:, k, :], ps_t[:], x_hi[par][:, k, :].bitcast(F32), ALU.subtract).then_inc(low_set, 1)

            def first_low(b, par):
                dve.wait_ge(p_high, b + 1)
                rows = slice(RANK, P)
                dve.tensor_tensor(pp[par][rows], ps_p[rows], pp[par][rows].bitcast(F32), ALU.subtract).then_inc(p_split, 1)

            def second_low(b, par):
                dve.wait_ge(q_high, b + 1)
                dve.tensor_tensor(q_lo[par][:], ps_q[:], q_hi[par][:].bitcast(F32), ALU.subtract).then_inc(q_low, 1)

            def add_x(b, par):
                dve.wait_ge(o_ready, b + 1)
                dve.wait_ge(xb_set, b + 1)
                wait(dve, stored[par], loads(b, par) - 16)
                dve.tensor_tensor(r[par][:], ps_o[:], xb[par][:], ALU.add).then_inc(r_set, 1)
                dve.wait_ge(r_set, b + 1)
                wait(dve, lnv_set, b - 1)
                for q in range(QT):
                    dve.bn_stats(bn[:, q, :], r[par][:, q, :]).then_inc(stats, 1)
                for q in range(QT):
                    dve.wait_ge(stats, QT * b + q + 1)
                    settle(dve, dve_settled)
                    dve.bn_aggr(mv[par][:, q, :], bn[:, q, :]).then_inc(aggr, 1)

            def layernorm(b, par):
                dve.wait_ge(lnr_set, b + 1)
                for q in range(QT):
                    dve.tensor_scalar(r[par][:, q, :], r[par][:, q, :], mv[par][:, q, 0:1], lnr[par][:, q:q + 1],
                                      ALU.subtract, ALU.mult).then_inc(out_set, 1)

            low(0, 0, 0)
            low(0, 0, 1)
            first_low(0, 0)

            def step(b, par):
                for k in range(HT):
                    dve.wait_ge(gelu_done, HT * b + k + 1)
                    if k < RING:
                        wait(dve, q_ready, HT * (b - 1) + HT - RING + k + 1)
                    else:
                        wait(dve, q_ready, HT * b + k - RING + 1)
                    dve.tensor_copy(h_hi[k % RING][:], hid[k % RING][:]).then_inc(hid_high, 1)
                    if k % 2 == 0:
                        dve.wait_ge(hid_high, HT * b + k + 1)
                        dve.tensor_tensor(h_lo[k % RING][:], hid[k % RING][:], h_hi[k % RING][:].bitcast(F32),
                                          ALU.subtract).then_inc(hid_low[0], 1)
                    if k == 2 and not (isinstance(b, int) and b == 0):
                        second_low(b - 1, 1 - par)
                    if k == 3 and not (isinstance(b, int) and b == 0):
                        add_x(b - 1, 1 - par)
                    if not is_last(b):
                        if k in (3, 4):
                            low(b + 1, 1 - par, k - 3)
                        if k == 6:
                            first_low(b + 1, 1 - par)
                if not (isinstance(b, int) and b == 0):
                    layernorm(b - 1, 1 - par)
            over(dve, B, step)
            second_low(B - 1, 1)
            add_x(B - 1, 1)
            layernorm(B - 1, 1)


def decoder_layer(nc, a, out):
    def scratch(name, shape, dt=F32):
        return nc.dram_tensor(name, shape, dt, kind="Internal").ap()

    gate_d = scratch("gate_d", (B, P, KT, T))
    filt_d = scratch("filt_d", (D, 2 * C))
    x1_d = scratch("x1_d", (B, P, QT, D))
    parts_d = scratch("parts_d", (2, 2, KT, 3, P, T), BF16)
    x2_d = scratch("x2_d", (B, P, QT, D))
    with nc.sbuf_tensor("xv_all", [P, B, G, NC], F32) as xv_all:
        project(nc, a["x"], a["w_in"], a["pre_w"], a["taps"], a["tap_bias"], a["c_ident"], xv_all, gate_d)
        longconv(nc, a["lp_rows"], a["lp_cols"], a["res_cols"], a["lp_chan"], a["res_chan"], a["skip"], a["c_left"],
                 a["c_ramp"], a["c_lag"], a["c_qmask"], a["c_gmask"], a["c_notfirst"], filt_d, xv_all)
        mlp(nc, a["x"], gate_d, a["w_out"], a["w_gate"], a["w_up"], a["w_down"], a["post_w"], a["c_ident"], xv_all, x1_d)
    attend(nc, x1_d, a["ctx_t"], a["w_qkcv"], a["w_ctx"], a["w_proj"], a["b_qkc"], a["b_ck"], a["b_rows"], a["c_ident"],
           a["c_heads"], a["c_sel"], parts_d, x2_d)
    ffn(nc, x2_d, a["w_u1"], a["w_v1"], a["b1"], a["w_u2"], a["w_v2"], a["b2"], a["c_ident"], out)


def layout(v):
    import numpy as np

    def get(name):
        return np.asarray(v[name])

    def tiles(w):
        return w.reshape(-1, P, w.shape[-1]).transpose(1, 0, 2)

    def cols(b):
        return b.reshape(-1, P).T

    spread = np.arange(D).reshape(KT, HE, HD).transpose(0, 2, 1).reshape(-1)
    lp = get("L0_attn_log_poles").reshape(D, S)
    res = get("L0_attn_residues")
    wx, bx = (lambda n: get("L0_xattn_W" + n)), (lambda n: get("L0_xattn_b" + n))
    return {
        "x": get("x"),
        "w_in": tiles(get("L0_attn_in_proj_w").T),
        "pre_w": cols(get("L0_attn_pre_norm_w")),
        "taps": tiles(get("L0_attn_short_w").reshape(3 * D, 3)),
        "tap_bias": cols(get("L0_attn_short_b")),
        "lp_rows": lp.reshape(KT, 4, C, S).transpose(1, 0, 2, 3),
        "lp_cols": lp.reshape(KT, 4, C // 2, 2, S).transpose(1, 3, 4, 0, 2).reshape(P, G // 2),
        "res_cols": res.reshape(KT, 4, C // 2, 2, S).transpose(1, 3, 4, 0, 2).reshape(P, G // 2),
        "lp_chan": tiles(lp),
        "res_chan": tiles(res),
        "skip": cols(get("L0_attn_D_skip")),
        "w_out": tiles(get("L0_attn_out_proj_w").T),
        "w_gate": tiles(get("L0_attn_l1_w").T),
        "w_up": tiles(get("L0_attn_l2_w").T),
        "w_down": get("L0_attn_l3_w").T.reshape(FT, FM, D).transpose(1, 0, 2),
        "post_w": cols(get("L0_attn_post_norm_w")),
        "ctx_t": get("ctx_512").transpose(2, 0, 1),
        "w_qkcv": np.stack([tiles(w) for w in (wx("q")[:, spread], wx("k")[:, spread], wx("cq"), wx("v"))]),
        "w_ctx": np.stack([wx("ck"), wx("cv")], 1),
        "w_proj": tiles(wx("p")),
        "b_qkc": np.stack([cols(b) for b in (bx("q")[spread], bx("k")[spread], bx("cq"))], 1),
        "b_ck": cols(bx("ck")),
        "b_rows": np.stack([bx("v"), bx("cv"), bx("p")]),
        "w_u1": tiles(get("L0_ffn_U1")),
        "w_v1": get("L0_ffn_V1"),
        "b1": cols(get("L0_ffn_b1")),
        "w_u2": tiles(get("L0_ffn_U2")),
        "w_v2": get("L0_ffn_V2"),
        "b2": get("L0_ffn_b2").reshape(1, D),
    }


def constants():
    import numpy as np
    f32 = np.float32
    p = np.arange(P)
    quarter, group = p // C, p // S % 2
    sel = np.zeros((H, HE, 2, CL), f32)
    for h in range(H):
        sel[h, h // 2, h % 2] = 1
    return {
        "c_ident": np.eye(P, dtype=f32),
        "c_left": (C - 1 - p % C).astype(f32)[:, None],
        "c_ramp": np.broadcast_to(np.arange(1, C + 1, dtype=f32), (P, C)),
        "c_lag": np.broadcast_to(np.arange(C, dtype=f32), (P, C)),
        "c_qmask": (quarter[:, None] == np.arange(4)).astype(f32),
        "c_gmask": ((quarter[:, None, None] == np.arange(4)) & (group[:, None, None] == np.arange(2)[:, None])).astype(f32),
        "c_notfirst": np.broadcast_to((np.arange(B * NC) % NC != 0).astype(f32), (P, B * NC)),
        "c_heads": (p[:, None] // HD == np.arange(HE)).astype(f32),
        "c_sel": sel.reshape(H, HE * P),
    }


def kernel(**inputs):
    import numpy as np
    import concourse.bacc as bacc
    from concourse.bass_utils import run_bass_kernel_spmd

    nc = bacc.Bacc("TRN2", target_bir_lowering=False, num_devices=1)
    arrays, aps = {}, {}
    for name, value in {**layout(inputs), **constants()}.items():
        value = np.ascontiguousarray(value)
        arrays[f"in_{name}"] = value
        aps[name] = nc.dram_tensor(f"in_{name}", value.shape, mybir.dt.from_np(value.dtype), kind="ExternalInput").ap()
    out = nc.dram_tensor("out", (B, T, D), F32, kind="ExternalOutput").ap()
    decoder_layer(nc, aps, out)
    run = run_bass_kernel_spmd(nc, [arrays], core_ids=[0])
    return run.results[0]["out"]
```
